# Optimizing a Trainium2 kernel written in Bass

```python
import numpy as np
import jax
import jax.numpy as jnp

def _softmax(x, axis=-1):
    return jax.nn.softmax(x, axis=axis)

def _gelu(x):
    return jax.nn.gelu(x, approximate=True)

def _silu(x):
    return jax.nn.silu(x)

def _sigmoid(x):
    return jax.nn.sigmoid(x)

def _layernorm(x, axis=-1, eps=1e-05):
    m = jnp.mean(x, axis=axis, keepdims=True)
    v = jnp.var(x, axis=axis, keepdims=True)
    return (x - m) / jnp.sqrt(v + eps)

def _scatter_add(tgt, idx, src, axis=0):
    return tgt.at[idx].add(src)

def _segment_sum(src, seg, n):
    return jax.ops.segment_sum(src, seg, n)
kernel_name = 'mk_hybrid_d1_jaxref_r4_23807b'

def setup_inputs(seed: int=0):
    np.random.seed(seed)
    _w = jnp.asarray

    def _L0_attn_a_setup():
        import math
        import jax, jax.numpy as jnp
        import numpy as np
        N_HEAD = 16
        key = jax.random.key(seed)
        k1, k2, k3, k4 = jax.random.split(key, 4)
        B, T, C, R = (4, 512, 256, 64)
        std = 0.02
        return {'hidden_states': jax.random.normal(k1, (B, T, C), dtype=jnp.float32), 'W_basis': jax.random.normal(k2, (R, C), dtype=jnp.float32) * std, 'W_v': jax.random.normal(k3, (C, C), dtype=jnp.float32) * std, 'b_v': jnp.zeros((C,), dtype=jnp.float32), 'W_o': jax.random.normal(k4, (C, C), dtype=jnp.float32) * std, 'b_o': jnp.zeros((C,), dtype=jnp.float32)}
    _L0_attn_a_in = _L0_attn_a_setup()

    def _L0_attn_b_setup():
        import jax, jax.numpy as jnp
        import numpy as np
        BASE_FREQUENCY = 10000.0
        LRP = 17
        MIN_L = 1.0 - LRP / 100.0
        SDT_L = (BASE_FREQUENCY - MIN_L * BASE_FREQUENCY) * 2.0
        ARM_ATTENTION = 2.0
        HEADS_DIM = 64

        def _nrope(xs, base, angle_range):
            N, T, d = xs.shape
            half = d // 2
            inv_freq = base ** (-jnp.arange(half, dtype=jnp.float32) / half)
            pos = jnp.arange(T, dtype=jnp.float32)
            scale = angle_range / jnp.maximum(T - 1, 1)
            ang = pos[:, None] * inv_freq[None, :] * scale
            cos, sin = (jnp.cos(ang), jnp.sin(ang))
            x1, x2 = (xs[..., :half], xs[..., half:])
            return jnp.concatenate([x1 * cos - x2 * sin, x1 * sin + x2 * cos], axis=-1)
        key = jax.random.key(seed)
        ks = jax.random.split(key, 9)
        B, T, E = (4, 256, 256)
        x = jax.random.normal(ks[0], (B, T, E), dtype=jnp.float32)

        def w(k):
            return jax.random.normal(k, (E, E), dtype=jnp.float32) * 0.02
        z = jnp.zeros((E,), dtype=jnp.float32)
        return {'x': x, 'Wq': w(ks[1]), 'bq': z, 'Wk': w(ks[2]), 'bk': z, 'Wv': w(ks[3]), 'bv': z, 'Wo': w(ks[4]), 'bo': z, 'nrope_freq': jnp.zeros((1,), dtype=jnp.float32)}
    _L0_attn_b_in = _L0_attn_b_setup()

    def _L0_ffn_setup():
        import jax, jax.numpy as jnp
        import numpy as np
        B, S, D = (4, 1024, 256)
        E, F_EXP = (16, 512)
        F_C = 2.0
        F_SH = 512
        key = jax.random.key(seed)
        ks = jax.random.split(key, 8)
        s = 0.02
        return {'hidden_states': jax.random.normal(ks[0], (B, S, D), jnp.float32), 'gate_w': jax.random.normal(ks[1], (E, D), jnp.float32) * s, 'Wg': jax.random.normal(ks[2], (E, F_EXP, D), jnp.float32) * s, 'Wu': jax.random.normal(ks[3], (E, F_EXP, D), jnp.float32) * s, 'Wd': jax.random.normal(ks[4], (E, D, F_EXP), jnp.float32) * s, 'Ws_g': jax.random.normal(ks[5], (F_SH, D), jnp.float32) * s, 'Ws_u': jax.random.normal(ks[6], (F_SH, D), jnp.float32) * s, 'Ws_d': jax.random.normal(ks[7], (D, F_SH), jnp.float32) * s}
    _L0_ffn_in = _L0_ffn_setup()
    _d = {'L0_attn_a_hidden_states': _L0_attn_a_in['hidden_states'], 'L0_attn_a_W_basis': _L0_attn_a_in['W_basis'], 'L0_attn_a_W_v': _L0_attn_a_in['W_v'], 'L0_attn_a_b_v': _L0_attn_a_in['b_v'], 'L0_attn_a_W_o': _L0_attn_a_in['W_o'], 'L0_attn_a_b_o': _L0_attn_a_in['b_o'], 'L0_attn_b_Wq': _L0_attn_b_in['Wq'], 'L0_attn_b_bq': _L0_attn_b_in['bq'], 'L0_attn_b_Wk': _L0_attn_b_in['Wk'], 'L0_attn_b_bk': _L0_attn_b_in['bk'], 'L0_attn_b_Wv': _L0_attn_b_in['Wv'], 'L0_attn_b_bv': _L0_attn_b_in['bv'], 'L0_attn_b_Wo': _L0_attn_b_in['Wo'], 'L0_attn_b_bo': _L0_attn_b_in['bo'], 'L0_attn_b_nrope_freq': _L0_attn_b_in['nrope_freq'], 'L0_ffn_gate_w': _L0_ffn_in['gate_w'], 'L0_ffn_Wg': _L0_ffn_in['Wg'], 'L0_ffn_Wu': _L0_ffn_in['Wu'], 'L0_ffn_Wd': _L0_ffn_in['Wd'], 'L0_ffn_Ws_g': _L0_ffn_in['Ws_g'], 'L0_ffn_Ws_u': _L0_ffn_in['Ws_u'], 'L0_ffn_Ws_d': _L0_ffn_in['Ws_d']}
    _x0 = _d['L0_attn_a_hidden_states']
    _d['L0_attn_a_hidden_states'] = jax.random.normal(jax.random.fold_in(jax.random.key(seed), 1), (8, 1024, 256), dtype=_x0.dtype)
    del _x0
    return _d

def reference(L0_attn_a_hidden_states, L0_attn_a_W_basis, L0_attn_a_W_v, L0_attn_a_b_v, L0_attn_a_W_o, L0_attn_a_b_o, L0_attn_b_Wq, L0_attn_b_bq, L0_attn_b_Wk, L0_attn_b_bk, L0_attn_b_Wv, L0_attn_b_bv, L0_attn_b_Wo, L0_attn_b_bo, L0_attn_b_nrope_freq, L0_ffn_gate_w, L0_ffn_Wg, L0_ffn_Wu, L0_ffn_Wd, L0_ffn_Ws_g, L0_ffn_Ws_u, L0_ffn_Ws_d):

    def _L0_attn_a_ref(hidden_states, W_basis, W_v, b_v, W_o, b_o):
        import math
        import jax, jax.numpy as jnp
        import numpy as np
        N_HEAD = 16
        B, T, C = hidden_states.shape
        nh = N_HEAD
        hd = C // nh
        R = W_basis.shape[0]
        latent = hidden_states @ W_basis.T
        v = hidden_states @ W_v.T + b_v
        v = v.reshape(B, T, nh, hd).transpose(0, 2, 1, 3)
        scores = jnp.einsum('bqr,bkr->bqk', latent, latent) * (1.0 / math.sqrt(R))
        causal = jnp.tril(jnp.ones((T, T), dtype=bool))
        scores = jnp.where(causal[None, :, :], scores, -jnp.inf)
        att = jax.nn.softmax(scores, axis=-1)
        y = jnp.einsum('bqk,bhkd->bhqd', att, v)
        y = y.transpose(0, 2, 1, 3).reshape(B, T, C)
        out = y @ W_o.T + b_o
        return out

    def _L0_attn_b_ref(x, Wq, bq, Wk, bk, Wv, bv, Wo, bo, nrope_freq):
        import jax, jax.numpy as jnp
        import numpy as np
        BASE_FREQUENCY = 10000.0
        LRP = 17
        MIN_L = 1.0 - LRP / 100.0
        SDT_L = (BASE_FREQUENCY - MIN_L * BASE_FREQUENCY) * 2.0
        ARM_ATTENTION = 2.0
        HEADS_DIM = 64

        def _nrope(xs, base, angle_range):
            N, T, d = xs.shape
            half = d // 2
            inv_freq = base ** (-jnp.arange(half, dtype=jnp.float32) / half)
            pos = jnp.arange(T, dtype=jnp.float32)
            scale = angle_range / jnp.maximum(T - 1, 1)
            ang = pos[:, None] * inv_freq[None, :] * scale
            cos, sin = (jnp.cos(ang), jnp.sin(ang))
            x1, x2 = (xs[..., :half], xs[..., half:])
            return jnp.concatenate([x1 * cos - x2 * sin, x1 * sin + x2 * cos], axis=-1)
        B, T, E = x.shape
        HD = HEADS_DIM
        H = E // HD
        half = HD // 2
        q = (x @ Wq + bq).reshape(B, T, H, HD).transpose(0, 2, 1, 3)
        k = (x @ Wk + bk).reshape(B, T, H, HD).transpose(0, 2, 1, 3)
        v = (x @ Wv + bv).reshape(B, T, H, HD).transpose(0, 2, 1, 3)
        q_content, q_spatial = (q[..., :half], q[..., half:])
        k_content, k_spatial = (k[..., :half], k[..., half:])
        base = jax.nn.sigmoid(nrope_freq[0]) * SDT_L + MIN_L * BASE_FREQUENCY
        rng = ARM_ATTENTION * jnp.pi
        q_spatial = _nrope(q_spatial.reshape(B * H, T, half), base, rng).reshape(B, H, T, half)
        k_spatial = _nrope(k_spatial.reshape(B * H, T, half), base, rng).reshape(B, H, T, half)
        q = jnp.concatenate([q_content, q_spatial], axis=-1)
        k = jnp.concatenate([k_content, k_spatial], axis=-1)
        score = jnp.einsum('bhqd,bhkd->bhqk', q, k) / jnp.sqrt(jnp.float32(HD))
        attn = jax.nn.softmax(score, axis=-1)
        out = jnp.einsum('bhqk,bhkd->bhqd', attn, v)
        out = out.transpose(0, 2, 1, 3).reshape(B, T, E)
        return out @ Wo + bo

    def _L0_ffn_ref(hidden_states, gate_w, Wg, Wu, Wd, Ws_g, Ws_u, Ws_d):
        import jax, jax.numpy as jnp
        import numpy as np
        B, S, D = (4, 1024, 256)
        E, F_EXP = (16, 512)
        F_C = 2.0
        F_SH = 512
        b, s, d = hidden_states.shape
        e = gate_w.shape[0]
        cap = int(s * F_C / e)
        logits = jnp.einsum('bsd,ed->bse', hidden_states, gate_w)
        scores = jax.nn.softmax(logits, axis=-1).transpose(0, 2, 1)
        topk_w, topk_idx = jax.lax.top_k(scores, cap)
        x_tok = jnp.take_along_axis(hidden_states[:, None, :, :], topk_idx[..., None], axis=2)
        g = jnp.einsum('becd,efd->becf', x_tok, Wg)
        u = jnp.einsum('becd,efd->becf', x_tok, Wu)
        h = jax.nn.gelu(g, approximate=False) * u
        eo = jnp.einsum('becf,edf->becd', h, Wd) * topk_w[..., None]
        offs = (jnp.arange(b) * s)[:, None, None]
        flat_idx = (topk_idx + offs).reshape(-1)
        flat = jnp.zeros((b * s, d), hidden_states.dtype)
        flat = flat.at[flat_idx].add(eo.reshape(-1, d))
        out = flat.reshape(b, s, d)
        gs = jnp.einsum('bsd,fd->bsf', hidden_states, Ws_g)
        us = jnp.einsum('bsd,fd->bsf', hidden_states, Ws_u)
        shared = jnp.einsum('bsf,df->bsd', jax.nn.gelu(gs, approximate=False) * us, Ws_d)
        return out + shared
    x = L0_attn_a_hidden_states
    x = x + _L0_attn_a_ref(_layernorm(x, axis=-1), L0_attn_a_W_basis, L0_attn_a_W_v, L0_attn_a_b_v, L0_attn_a_W_o, L0_attn_a_b_o)
    x = x + _L0_ffn_ref(_layernorm(x, axis=-1), L0_ffn_gate_w, L0_ffn_Wg, L0_ffn_Wu, L0_ffn_Wd, L0_ffn_Ws_g, L0_ffn_Ws_u, L0_ffn_Ws_d)
    x = x + _L0_attn_b_ref(_layernorm(x, axis=-1), L0_attn_b_Wq, L0_attn_b_bq, L0_attn_b_Wk, L0_attn_b_bk, L0_attn_b_Wv, L0_attn_b_bv, L0_attn_b_Wo, L0_attn_b_bo, L0_attn_b_nrope_freq)
    x = x + _L0_ffn_ref(_layernorm(x, axis=-1), L0_ffn_gate_w, L0_ffn_Wg, L0_ffn_Wu, L0_ffn_Wd, L0_ffn_Ws_g, L0_ffn_Ws_u, L0_ffn_Ws_d)
    return x

_drawn_inputs = setup_inputs


def setup_inputs(seed=0):
    import zlib

    import numpy as np

    out = dict(_drawn_inputs(seed))
    spreads = {'L0_attn_a_b_v': (0.0, 0.1),
     'L0_attn_a_b_o': (0.0, 0.1),
     'L0_attn_b_bq': (0.0, 0.8),
     'L0_attn_b_bk': (0.0, 2.0),
     'L0_attn_b_bv': (0.0, 0.478),
     'L0_attn_b_bo': (0.0, 0.285)}
    factors = {'L0_attn_a_W_basis': 8.0,
     'L0_attn_a_W_v': 5.254,
     'L0_attn_b_Wq': 8.0,
     'L0_attn_b_Wk': 8.0,
     'L0_attn_b_Wv': 5.163,
     'L0_ffn_gate_w': 8.0,
     'L0_ffn_Wg': 7.933,
     'L0_ffn_Wu': 7.766,
     'L0_ffn_Wd': 7.742,
     'L0_ffn_Ws_g': 4.05,
     'L0_ffn_Ws_u': 3.917,
     'L0_ffn_Ws_d': 3.831}
    for name, (base, spread) in spreads.items():
        noise = np.random.default_rng([zlib.crc32(name.encode()), seed]).standard_normal(out[name].shape)
        drawn = base * np.exp(spread * noise) if base else spread * noise
        out[name] = jnp.asarray(drawn.astype(out[name].dtype))
    for name, factor in factors.items():
        out[name] = (out[name] * factor).astype(out[name].dtype)
    return out
```

```python
from contextlib import ExitStack

import concourse.bass as bass
from concourse import mybir
from concourse.alu_op_type import AluOpType as ALU

ACT = mybir.ActivationFunctionType
AX = mybir.AxisListType
F32 = mybir.dt.float32
F32R = mybir.dt.float32r
BF16 = mybir.dt.bfloat16
U32 = mybir.dt.uint32

P = 128
B, S, D = 8, 1024, 256
T = S // P
KD = D // P
BANK = 512
HALVES = S // BANK
TH = BANK // P
E, F = 16, 512
CAP = S * 2 // E
EPS = 1e-5


class Ring:

    def __init__(self, sem, name, views, keys, before=(), iterations=B, not_first=()):
        n = len(views)
        assert len(keys) % n == 0 and len(before) % n == 0
        self.before = list(before)
        self.views = views
        self.full_of = [sem(f"{name}_full{s}") for s in range(n)]
        self.emptied_of = [sem(f"{name}_emptied{s}") for s in range(n)]
        self.at = {key: k for k, key in enumerate(keys)}
        assert len(self.at) == len(keys)
        self.iterations, self.not_first = iterations, not_first
        self.skipped_at = self.at[self.before[0]] if self.before else len(keys)
        self.n, self.per = n, len(keys) // n

    def view(self, key):
        return self.views[self.at[key] % self.n]

    def full(self, key):
        return self.full_of[self.at[key] % self.n]

    def emptied(self, key):
        return self.emptied_of[self.at[key] % self.n]

    def uses(self, key, i):
        if isinstance(i, int) and i == self.iterations - 1 and self.at[key] >= self.skipped_at:
            return i * self.per + self.at[key] // self.n
        if self.not_first:
            if isinstance(i, int) and i == 0:
                return [k for k in self.at if k not in self.not_first].index(key) // self.n
            return i * self.per - len(self.not_first) // self.n + self.at[key] // self.n
        return i * self.per + len(self.before) // self.n + self.at[key] // self.n

    def uses_ahead(self, key, i):
        if isinstance(i, int) and i == 0:
            return self.before.index(key) // self.n
        return i * self.per + (len(self.before) // self.n - self.per + self.at[key] // self.n)


def spread(row, *shape):
    return row.partition_broadcast(P)


def high(ap):
    return ap.bitcast(F32)


def three_products(pe, out, lhs, lhs_low, rhs, rhs_low, ks, last=True, first=True):
    n = 0
    total = 3 * len(ks)
    for k in ks:
        for a, b in ((lhs, rhs), (lhs, rhs_low), (lhs_low, rhs)):
            ins = pe.matmul(out, a(k), b(k), start=(first and n == 0), stop=(last and n == total - 1))
            n += 1
    return ins


class Frame:

    def __init__(self, nc, ctx, tag, x_in, x_out, xn_out, ident, gate, scores, one_norm=False, slots=2):
        self.nc, self.x_in, self.x_out, self.xn_out = nc, x_in, x_out, xn_out
        self.ident, self.gate, self.scores = ident, gate, scores

        def sb(name, shape, dt=F32):
            return ctx.enter_context(nc.sbuf_tensor(f"{tag}_{name}", shape, dt))

        def sem(name):
            return ctx.enter_context(nc.semaphore(f"{tag}_{name}"))

        self.sb, self.sem = sb, sem
        self.slots, self.lead = slots, slots // 2
        self.x = sb("x", [P, slots, T, D])
        self.xn = sb("xn", [P, T, D])
        self.xt_high = sb("xt_high", [P, KD, S], F32R)
        self.xt_low = sb("xt_low", [P, KD, S], F32R)
        self.bias_out = sb("bias_out", [P, D])
        self.stats = sb("stats", [P, T, 6])
        self.mv = sb("mv", [P, T, 2])
        self.rstd = sb("rstd", [P, T])
        self.minus_half = sb("minus_half", [P, T])
        self.one_norm = one_norm
        self.xn2 = self.xn if one_norm else sb("xn2", [P, T, D])
        self.stats2 = sb("stats2", [P, T, 6])
        self.mv2 = sb("mv2", [P, T, 2])
        self.rstd2 = sb("rstd2", [P, T])
        self.xn2t = sb("xn2t", [P, KD, P])
        self.logits = sb("logits", [P, T, E])
        self.shifted = sb("shifted", [P, T, E])
        self.expd = sb("expd", [P, T, E])
        self.peak = sb("peak", [P, T])
        self.total = sb("total", [P, T])
        self.share = sb("share", [P, T])

        self.x_loaded = sem("x_loaded")
        self.passed = sem("passed")
        self.half_set = sem("half_set")
        self.stats_done = sem("stats_done")
        self.mv_done = sem("mv_done")
        self.var_done = sem("var_done")
        self.rstd_done = sem("rstd_done")
        self.xn_ready = sem("xn_ready")
        self.xb_ready = sem("xb_ready")
        self.xt_high_ready = sem("xt_high_ready")
        self.out_added = sem("out_added")
        self.x1_stored = sem("x1_stored")
        self.xn_stored = sem("xn_stored")
        self.xn2_free = sem("xn2_free")
        self.stats2_done = sem("stats2_done")
        self.mv2_done = sem("mv2_done")
        self.var2_done = sem("var2_done")
        self.rstd2_done = sem("rstd2_done")
        self.xn2_ready = sem("xn2_ready")
        self.centred2 = sem("centred2")
        self.peak_done = sem("peak_done")
        self.shifted_done = sem("shifted_done")
        self.exp_done = sem("exp_done")
        self.total_done = sem("total_done")
        self.share_done = sem("share_done")
        self.scores_done = sem("scores_done")

    def memory(self, psum_bank):
        self.out = psum_bank[:, 0:D]
        self.turn = psum_bank[:, D:2 * D].rearrange("p (k t) -> p k t", k=KD)
        self.lg = psum_bank[:, D:D + E]
        self.out_full = self.sem("out_full")
        self.turn_full = self.sem("turn_full")
        self.turned = self.sem("turned")
        self.logits_full = self.sem("logits_full")
        self.logits_taken = self.sem("logits_taken")

    def sp_load(self, sp, i):
        sp.dma_start(self.x[:, bass.ds(i % self.slots, 1), :, :].rearrange("p a t d -> p (a t) d"),
                     self.x_in[bass.ds(i, 1)].rearrange("a (t p) d -> p (a t) d", p=P)).then_inc(self.x_loaded, 16)

    def sp_store_x1(self, sp, i):
        sp.wait_ge(self.out_added, T * (i + 1))
        sp.sem_inc(self.passed, 1)
        sp.dma_start(self.x_out[bass.ds(i, 1)].rearrange("a (t p) d -> p (a t) d", p=P),
                     self.x[:, bass.ds(i % self.slots, 1), :, :].rearrange("p a t d -> p (a t) d")).then_inc(self.x1_stored, 16)

    def sp_store_xn(self, sp, r):
        sp.wait_ge(self.xn2_ready, T * (r + 1))
        sp.sem_inc(self.passed, 1)
        sp.dma_start(self.xn_out[bass.ds(r, 1)].rearrange("a (t p) d -> p (a t) d", p=P),
                     self.xn2[:, :, :]).then_inc(self.xn_stored, 16)

    def sp_all(self, sp, more=lambda i: None):
        sp.sem_inc(self.xn2_free, 1)
        for i in range(1, self.lead + 1):
            sp.wait_ge(self.x_loaded, 16 * i)
            self.sp_load(sp, i)
        more(0)

        def batch(i, ahead):
            if ahead and self.lead > 1:
                sp.wait_ge(self.x_loaded, 16 * (i + self.lead))
                sp.sem_inc(self.passed, 1)
                self.sp_load(sp, i + self.lead)
            self.sp_store_x1(sp, i - 1)
            more(i)
            sp.wait_ge(self.x1_stored, 16 * i)
            sp.sem_inc(self.passed, 1)
            sp.wait_ge(self.stats2_done, T * i)
            sp.wait_ge(self.xn2_ready, T * i)
            if ahead and self.lead == 1:
                sp.wait_ge(self.x_loaded, 16 * (i + 1))
                sp.sem_inc(self.passed, 1)
                self.sp_load(sp, i + 1)
            self.sp_store_xn(sp, i - 1)
            sp.wait_ge(self.xn_stored, 16 * i)
            sp.sem_inc(self.xn2_free, 1)
        with sp.Fori(1, B - self.lead) as i:
            batch(i, True)
        for i in range(B - self.lead, B):
            batch(i, False)
        self.sp_store_x1(sp, B - 1)
        self.sp_store_xn(sp, B - 1)
        sp.wait_ge(self.x1_stored, 16 * B)
        sp.wait_ge(self.xn_stored, 16 * B)

    def dve_stats(self, dve, i, ts):
        dve.wait_ge(self.x_loaded, 16 * (i + 1))
        dve.sem_inc(self.passed, 1)
        for t in ts:
            dve.bn_stats(self.stats[:, t, :],
                         self.x[:, bass.ds(i % self.slots, 1), t, :]).then_inc(self.stats_done, 1)

    def dve_mean(self, dve, i):
        dve.wait_ge(self.stats_done, T * (i + 1))
        dve.sem_inc(self.passed, 1)
        for t in range(T):
            dve.bn_aggr(self.mv[:, t, :], self.stats[:, t, :]).then_inc(self.mv_done, 1)

    def pool_rstd(self, pool, i):
        pool.wait_ge(self.mv_done, T * (i + 1))
        pool.sem_inc(self.passed, 1)
        pool.tensor_scalar(self.rstd[:, :], self.mv[:, :, 1], EPS, None, ALU.add).then_inc(self.var_done, 1)
        pool.wait_ge(self.var_done, i + 1)
        pool.tensor_tensor(self.rstd[:, :], self.rstd[:, :], self.minus_half[:, :], ALU.pow)\
            .then_inc(self.rstd_done, 1)

    def dve_norm(self, dve, i, ts):
        dve.wait_ge(self.rstd_done, i + 1)
        if self.one_norm and not isinstance(i, int):
            dve.wait_ge(self.xn2_free, i)
        for t in ts:
            dve.tensor_scalar(self.xn[:, t, :], self.x[:, bass.ds(i % self.slots, 1), t, :],
                              self.mv[:, t, 0:1], self.rstd[:, t:t + 1],
                              ALU.subtract, ALU.mult).then_inc(self.xn_ready, 1)

    def pool_bias(self, pool, i):
        pool.wait_ge(self.xn_ready, T * (i + 1))
        for t in range(T):
            x = self.x[:, bass.ds(i % self.slots, 1), t, :]
            pool.tensor_tensor(x, x, self.bias_out[:, :].unsqueeze(1), ALU.add).then_inc(self.xb_ready, 1)

    def pe_turn(self, pe, ring, i, h):
        key = ("x", h)
        pe.wait_ge(ring.emptied(key), ring.uses_ahead(key, i))
        pe.wait_ge(self.xn_ready, T * i + TH * (h + 1))
        for k in range(KD):
            for t in range(TH):
                ins = pe.transpose(ring.view(key)[:, k * BANK + t * P:k * BANK + (t + 1) * P],
                                   self.xn[:, TH * h + t, k * P:(k + 1) * P], self.ident[:, :])
        ins.then_inc(ring.full(key), 1)

    def act_turn(self, act, ring, i, h):
        key = ("x", h)
        act.wait_ge(ring.full(key), ring.uses_ahead(key, i) + 1)
        act.activation(self.xt_high[:, :, h * BANK:(h + 1) * BANK],
                       ring.view(key).rearrange("p (k s) -> p k s", k=KD), ACT.Copy).then_inc(self.xt_high_ready, 1)

    def dve_turn(self, dve, ring, i, h):
        key = ("x", h)
        dve.wait_ge(self.xt_high_ready, HALVES * i + h + 1)
        cols = slice(h * BANK, (h + 1) * BANK)
        dve.tensor_tensor(self.xt_low[:, :, cols], ring.view(key).rearrange("p (k s) -> p k s", k=KD),
                          high(self.xt_high[:, :, cols]), ALU.subtract).then_inc(ring.emptied(key), 1)

    def pe_wait_turned(self, pe, ring, i, h):
        key = ("x", h)
        pe.wait_ge(ring.emptied(key), ring.uses_ahead(key, i) + 1)

    def pe_out(self, pe, i, t, y, w):
        pe.wait_ge(self.out_added, T * i + t)
        for k in range(KD):
            ins = pe.matmul(self.out, y(k), w(k), start=(k == 0), stop=(k == KD - 1))
        ins.then_inc(self.out_full, 1)

    def dve_out(self, dve, i, t):
        dve.wait_ge(self.out_full, T * i + t + 1)
        dve.wait_ge(self.xb_ready, T * i + t + 1)
        x = self.x[:, bass.ds(i % self.slots, 1), t, :]
        dve.tensor_tensor(x, self.out.unsqueeze(1), x, ALU.add).then_inc(self.out_added, 1)

    def pe_outs(self, pe, ring, i, key, ts, y, w):
        pe.wait_ge(ring.emptied(key), ring.uses(key, i))
        for n, t in enumerate(ts):
            for k in range(KD):
                ins = pe.matmul(ring.view(key)[:, n * D:(n + 1) * D], y(t, k), w(k), start=(k == 0), stop=(k == KD - 1))
        ins.then_inc(ring.full(key), 1)

    def dve_outs(self, dve, ring, i, key, ts):
        dve.wait_ge(ring.full(key), ring.uses(key, i) + 1)
        dve.wait_ge(self.xb_ready, T * (i + 1))
        x = self.x[:, bass.ds(i % self.slots, 1), ts[0]:ts[-1] + 1, :].rearrange("p a t d -> p (a t) d")
        dve.tensor_tensor(x, ring.view(key)[:, 0:len(ts) * D].rearrange("p (t d) -> p t d", d=D), x, ALU.add)\
            .then_inc(self.out_added, len(ts))

    def dve_outs_done(self, dve, ring, i, key, ts):
        dve.wait_ge(self.out_added, T * i + ts[-1] + 1)
        dve.sem_inc(ring.emptied(key), 1)

    def dve_stats2(self, dve, r, t):
        dve.wait_ge(self.out_added, T * r + t + 1)
        dve.sem_inc(self.passed, 1)
        dve.bn_stats(self.stats2[:, t, :], self.x[:, bass.ds(r % self.slots, 1), t, :]).then_inc(self.stats2_done, 1)

    def dve_mean2(self, dve, r):
        dve.wait_ge(self.stats2_done, T * (r + 1))
        dve.sem_inc(self.passed, 1)
        for t in range(T):
            dve.bn_aggr(self.mv2[:, t, :], self.stats2[:, t, :]).then_inc(self.mv2_done, 1)

    def pool_rstd2(self, pool, r):
        pool.wait_ge(self.mv2_done, T * (r + 1))
        pool.sem_inc(self.passed, 1)
        pool.tensor_scalar(self.rstd2[:, :], self.mv2[:, :, 1], EPS, None, ALU.add).then_inc(self.var2_done, 1)
        pool.wait_ge(self.var2_done, r + 1)
        pool.tensor_tensor(self.rstd2[:, :], self.rstd2[:, :], self.minus_half[:, :], ALU.pow)\
            .then_inc(self.rstd2_done, 1)

    def dve_norm2(self, dve, r, ts):
        dve.wait_ge(self.rstd2_done, r + 1)
        dve.wait_ge(self.xn2_free, r + 1)
        for t in ts:
            dve.tensor_scalar(self.xn2[:, t, :], self.x[:, bass.ds(r % self.slots, 1), t, :],
                              self.mv2[:, t, 0:1], self.rstd2[:, t:t + 1],
                              ALU.subtract, ALU.mult).then_inc(self.xn2_ready, 1)

    def pool_norm2(self, pool, r):
        pool.wait_ge(self.rstd2_done, r + 1)
        pool.wait_ge(self.xn2_free, r + 1)
        pool.sem_inc(self.passed, 1)
        pairs = [slice(t, t + 2) for t in range(0, T, 2)]
        for n in range(len(pairs) + 1):
            if n < len(pairs):
                ts = pairs[n]
                x = self.x[:, bass.ds(r % self.slots, 1), ts, :].rearrange("p a t d -> p (a t) d")
                pool.tensor_tensor(self.xn2[:, ts, :], x, self.mv2[:, ts, 0:1].to_broadcast([P, 2, D]),
                                   ALU.subtract).then_inc(self.centred2, 1)
            if n > 0:
                ts = pairs[n - 1]
                pool.wait_ge(self.centred2, len(pairs) * r + n)
                pool.tensor_tensor(self.xn2[:, ts, :], self.xn2[:, ts, :],
                                   self.rstd2[:, ts].unsqueeze(2).to_broadcast([P, 2, D]), ALU.mult)\
                    .then_inc(self.xn2_ready, 2)

    def pe_route_turn(self, pe, r, t):
        pe.wait_ge(self.xn2_ready, T * r + t + 1)
        if t > 0:
            pe.wait_ge(self.logits_taken, T * r + t)
        for k in range(KD):
            ins = pe.transpose(self.turn[:, k, :], self.xn2[:, t, k * P:(k + 1) * P], self.ident[:, :])
        ins.then_inc(self.turn_full, 1)

    def act_route_turn(self, act, r, t):
        act.wait_ge(self.turn_full, T * r + t + 1)
        act.activation(self.xn2t[:, :, :], self.turn, ACT.Copy).then_inc(self.turned, 1)

    def pe_route_logits(self, pe, r, t):
        pe.wait_ge(self.turned, T * r + t + 1)
        for k in range(KD):
            ins = pe.matmul(self.lg, self.xn2t[:, k, :], self.gate[:, k, :], start=(k == 0), stop=(k == KD - 1))
        ins.then_inc(self.logits_full, 1)

    def dve_route_logits(self, dve, r, t):
        dve.wait_ge(self.logits_full, T * r + t + 1)
        dve.tensor_copy(self.logits[:, t, :], self.lg).then_inc(self.logits_taken, 1)

    def last_route(self, banks, room, sems, before=0):
        self.last_banks = banks
        self.last_turned = room.rearrange("p h (t k s) -> p h t k s", k=KD, s=P)
        self.last_full, self.last_copied, self.last_logits_full, self.last_logits_taken = sems
        self.last_before = before

    def pe_last_route(self, pe):
        pe.wait_ge(self.out_added, T * B)
        for h in range(HALVES):
            pe.wait_ge(self.xn2_ready, T * (B - 1) + TH * (h + 1))
            for t in range(TH):
                for k in range(KD):
                    n = KD * t + k
                    ins = pe.transpose(self.last_banks[h][:, n * P:(n + 1) * P],
                                       self.xn2[:, TH * h + t, k * P:(k + 1) * P], self.ident[:, :])
            ins.then_inc(self.last_full, 1)
        for h in range(HALVES):
            pe.wait_ge(self.last_copied, self.last_before + h + 1)
            for t in range(TH):
                for k in range(KD):
                    ins = pe.matmul(self.last_banks[h][:, t * E:(t + 1) * E], self.last_turned[:, h, t, k, :],
                                    self.gate[:, k, :], start=(k == 0), stop=(k == KD - 1))
            ins.then_inc(self.last_logits_full, 1)

    def act_last_route(self, act):
        for h in range(HALVES):
            act.wait_ge(self.last_full, self.last_before + h + 1)
            act.activation(self.last_turned[:, h, :, :, :].rearrange("p t k s -> p (t k s)"),
                           self.last_banks[h][:, :], ACT.Copy).then_inc(self.last_copied, 1)

    def dve_last_route(self, dve):
        for h in range(HALVES):
            dve.wait_ge(self.last_logits_full, self.last_before + h + 1)
            dve.tensor_copy(self.logits[:, TH * h:TH * (h + 1), :],
                            self.last_banks[h][:, 0:TH * E].rearrange("p (t e) -> p t e", e=E))\
                .then_inc(self.last_logits_taken, 1)
        dve.wait_ge(self.last_logits_taken, self.last_before + HALVES)

    def dve_softmax(self, dve, r):
        dve.tensor_reduce(self.peak[:, :], self.logits[:, :, :], AX.X, ALU.max).then_inc(self.peak_done, 1)
        dve.wait_ge(self.peak_done, r + 1)
        dve.tensor_tensor(self.shifted[:, :, :], self.logits[:, :, :],
                          self.peak[:, :].unsqueeze(2).to_broadcast([P, T, E]), ALU.subtract)\
            .then_inc(self.shifted_done, 1)

    def act_softmax(self, act, r):
        act.wait_ge(self.shifted_done, r + 1)
        act.activation(self.expd[:, :, :], self.shifted[:, :, :], ACT.Exp).then_inc(self.exp_done, 1)

    def dve_scores(self, dve, r):
        dve.wait_ge(self.exp_done, r + 1)
        dve.tensor_reduce(self.total[:, :], self.expd[:, :, :], AX.X, ALU.add).then_inc(self.total_done, 1)
        dve.wait_ge(self.total_done, r + 1)
        dve.reciprocal(self.share[:, :], self.total[:, :]).then_inc(self.share_done, 1)
        dve.wait_ge(self.share_done, r + 1)
        dve.tensor_tensor(self.scores[:, :, bass.ds(r, 1), :].rearrange("p t a e -> p t (a e)"),
                          self.expd[:, :, :],
                          self.share[:, :].unsqueeze(2).to_broadcast([P, T, E]), ALU.mult)\
            .then_inc(self.scores_done, 1)


R = 64


def attention_a(nc, x_in, w_basis_t, w_v_t, b_v, w_o_t, b_o, x_out, xn_out, ident, mask, gate, scores):
    with ExitStack() as ctx:
        f = Frame(nc, ctx, "a", x_in, x_out, xn_out, ident, gate, scores, slots=4)
        sb, sem = f.sb, f.sem
        raw = sb("raw", [P, KD, P + D])
        w_high = sb("w_high", [P, KD, P + D], F32R)
        w_low = sb("w_low", [P, KD, P + D], F32R)
        w_out = sb("w_out", [P, KD, D])
        bias_v = sb("bias_v", [P, D])
        lat_high = sb("lat_high", [P, S], F32R)
        lat_low = sb("lat_low", [P, S], F32R)
        lat_both = sb("lat_both", [P, S], F32R)
        v = sb("v", [P, T, D])
        peak = sb("row_peak", [P, T])
        shift = sb("row_shift", [P, T])
        total = sb("row_total", [P, T])
        share = sb("row_share", [P, T])
        prob = sb("prob", [P, 2, S])
        prob_t = sb("prob_t", [P, 2, T, P])
        y = sb("y", [P, 2, D])
        yt = sb("yt", [P, 2, KD, P])

        def bank(name, n=1):
            return ctx.enter_context(nc.psum_tensor(f"a_bank_{name}", [P, n * BANK], F32))

        s_banks = [bank(f"s{n}", 2) for n in range(2)]
        t_banks = [bank(f"t{n}") for n in range(2)]
        y_bank = bank("y")
        f.memory(bank("out"))
        f.last_route(s_banks, prob[:, :, :], (f.turn_full, f.turned, f.logits_full, f.logits_taken), T * (B - 1))

        STEPS = T + 4

        def blocks(q):
            return [range(j, min(j + 4, q + 1)) for j in range(0, q + 1, 4)]

        def routed(s):
            return {0: (), 1: (0,), 2: (1,), 3: (2, 3)}.get(s, (s,))

        t_keys = []
        for s in range(STEPS):
            if 0 <= s - 1 < T:
                t_keys += [("p", s - 1, n) for n in range(len(blocks(s - 1)))]
            if 0 <= s - 3 < T:
                t_keys.append(("y", s - 3))
        ring_t = Ring(sem, "t", [b[:, :] for b in t_banks], t_keys)
        ring_s = Ring(sem, "s", [b[:, :] for b in s_banks],
                      [("l", h) for h in range(HALVES)] + [("v", n) for n in range(2)] + [("s", q) for q in range(T)]
                      + [("x", h) for h in range(HALVES)], before=[("x", h) for h in range(HALVES)])
        y_full, y_emptied = sem("y_full"), sem("y_emptied")
        w_loaded, w_high_ready, w_ready = sem("w_loaded"), sem("w_high_ready"), sem("w_ready")
        lat_high_ready = sem("lat_high_ready")
        peak_done, shift_done, share_done = sem("row_peak_done"), sem("row_shift_done"), sem("row_share_done")

        block = ctx.enter_context(nc.Block())

        @block.sync
        def _(sp):
            f.sp_load(sp, 0)
            for half in range(2):
                sp.dma_start(raw[:, :, half * R:(half + 1) * R],
                             w_basis_t.rearrange("(k p) r -> p k r", p=P)).then_inc(w_loaded, 16)
            sp.dma_start(raw[:, :, P:P + D], w_v_t.rearrange("(k p) c -> p k c", p=P)).then_inc(w_loaded, 16)
            sp.dma_start(w_out[:, :, :], w_o_t.rearrange("(k p) c -> p k c", p=P)).then_inc(w_loaded, 16)
            sp.dma_start(bias_v[:, :], spread(b_v)).then_inc(w_loaded, 16)
            sp.dma_start(f.bias_out[:, :], spread(b_o)).then_inc(w_loaded, 16)
            f.sp_all(sp)

        @block.gpsimd
        def _(pool):
            pool.memset(f.minus_half[:, :], -0.5).then_inc(f.half_set, 1)
            pool.wait_ge(f.half_set, 1)
            pool.wait_ge(w_loaded, 96)

            def ahead(i):
                f.pool_rstd(pool, i)
                f.pool_bias(pool, i)
            ahead(0)
            ahead(1)
            with pool.Fori(1, B - 1) as i:
                f.pool_rstd2(pool, i - 1)
                ahead(i + 1)
            for i in (B - 2, B - 1):
                f.pool_rstd2(pool, i)


        @block.scalar
        def _(act):
            def latents(i, h):
                key, cols = ("l", h), slice(h * BANK, (h + 1) * BANK)
                act.wait_ge(ring_s.full(key), ring_s.uses(key, i) + 1)
                act.activation(lat_both[0:R, cols], ring_s.view(key)[0:R, 0:BANK], ACT.Copy)\
                    .then_inc(lat_high_ready, 1)
                act.activation(lat_high[:, cols], ring_s.view(key)[:, 0:BANK], ACT.Copy)\
                    .then_inc(lat_high_ready, 1)

            def exps(i, q):
                key, n = ("s", q), (q + 1) * P
                act.wait_ge(shift_done, T * i + q + 1)
                if q >= 2:
                    last = ("p", q - 2, len(blocks(q - 2)) - 1)
                    act.wait_ge(ring_t.full(last), ring_t.uses(last, i) + 1)
                act.activation(prob[:, q % 2, 0:n], ring_s.view(key)[:, 0:n], ACT.Exp,
                               bias=shift[:, q:q + 1], scale=R ** -0.5,
                               accum_out=total[:, q:q + 1]).then_inc(ring_s.emptied(key), 1)

            def prob_turned(i, q):
                for n, js in enumerate(blocks(q)):
                    if n % 2 == 0:
                        key = ("p", q, n)
                        act.wait_ge(ring_t.full(key), ring_t.uses(key, i) + 1)
                        act.activation(prob_t[:, q % 2, js[0]:js[-1] + 1, :],
                                       ring_t.view(key)[:, 0:len(js) * P].rearrange("p (j t) -> p j t", t=P),
                                       ACT.Copy).then_inc(ring_t.emptied(key), 1)

            def y_turned(i, q):
                key = ("y", q)
                act.wait_ge(ring_t.full(key), ring_t.uses(key, i) + 1)
                act.activation(yt[:, q % 2, :, :], ring_t.view(key)[:, 0:D].rearrange("p (k t) -> p k t", t=P),
                               ACT.Copy).then_inc(ring_t.emptied(key), 1)

            def step(i, s):
                if 0 <= s - 1 < T:
                    prob_turned(i, s - 1)
                if 0 <= s - 3 < T:
                    y_turned(i, s - 3)

            def batch(i, before, ahead):
                if before:
                    step(i - 1, T)
                latents(i, 0)
                if before:
                    step(i - 1, T + 1)
                latents(i, 1)
                if before:
                    step(i - 1, T + 2)
                for s in range(T):
                    if s > 0:
                        prob_turned(i, s - 1)
                    if before and routed(s):
                        f.act_route_turn(act, i - 1, routed(s)[0])
                    exps(i, s)
                    if s >= 3:
                        y_turned(i, s - 3)
                    if before and len(routed(s)) > 1:
                        f.act_route_turn(act, i - 1, routed(s)[1])
                if before:
                    f.act_softmax(act, i - 1)
                for h in range(HALVES):
                    if ahead:
                        f.act_turn(act, ring_s, i + 1, h)
            act.wait_ge(w_loaded, 96)
            act.activation(w_high[:, :, :], raw[:, :, :], ACT.Copy).then_inc(w_high_ready, 1)
            for h in range(HALVES):
                f.act_turn(act, ring_s, 0, h)
            batch(0, False, True)
            with act.Fori(1, B - 1) as i:
                batch(i, True, True)
            batch(B - 1, True, False)
            for s in range(T, STEPS):
                step(B - 1, s)
            f.act_last_route(act)
            f.act_softmax(act, B - 1)

        @block.tensor
        def _(pe):
            def latents(i, h):
                f.pe_wait_turned(pe, ring_s, i, h)
                key, cols = ("l", h), slice(h * BANK, (h + 1) * BANK)
                pe.wait_ge(ring_s.emptied(key), ring_s.uses(key, i))
                three_products(pe, ring_s.view(key)[:, 0:BANK],
                               lambda k: w_high[:, k, 0:P], lambda k: w_low[:, k, 0:P],
                               lambda k: f.xt_high[:, k, cols], lambda k: f.xt_low[:, k, cols],
                               range(KD)).then_inc(ring_s.full(key), 1)

            def value_rows(i, n):
                key = ("v", n)
                pe.wait_ge(ring_s.emptied(key), ring_s.uses(key, i))
                for t in range(4):
                    rows = slice((4 * n + t) * P, (4 * n + t + 1) * P)
                    ins = three_products(pe, ring_s.view(key)[:, t * D:(t + 1) * D],
                                         lambda k: f.xt_high[:, k, rows], lambda k: f.xt_low[:, k, rows],
                                         lambda k: w_high[:, k, P:P + D], lambda k: w_low[:, k, P:P + D],
                                         range(KD))
                ins.then_inc(ring_s.full(key), 1)

            def scores_of(i, q):
                if q == 0 or q == T // 2:
                    key = ("l", 2 * q // T)
                    pe.wait_ge(ring_s.emptied(key), ring_s.uses(key, i) + 1)
                key, n = ("s", q), (q + 1) * P
                pe.wait_ge(ring_s.emptied(key), ring_s.uses(key, i))
                rows = slice(q * P, (q + 1) * P)
                for c in range(0, n, BANK):
                    e = min(c + BANK, n)
                    out = ring_s.view(key)[:, c:e]
                    pe.matmul(out, lat_high[:, rows], lat_both[:, c:e], start=True, stop=False)
                    ins = pe.matmul(out, lat_low[:, rows], lat_both[:, c:e], start=False, stop=True)
                pe.matmul(ring_s.view(key)[:, q * P:n], mask[:, 0, :], mask[:, 1, :], start=False, stop=True,
                          skip_group_check=True).then_inc(ring_s.full(key), 1)

            def turn_prob(i, q):
                key = ("s", q)
                pe.wait_ge(ring_s.emptied(key), ring_s.uses(key, i) + 1)
                for n, js in enumerate(blocks(q)):
                    key = ("p", q, n)
                    pe.wait_ge(ring_t.emptied(key), ring_t.uses(key, i))
                    for c, j in enumerate(js):
                        ins = pe.transpose(ring_t.view(key)[:, c * P:(c + 1) * P],
                                           prob[:, q % 2, j * P:(j + 1) * P], ident[:, :])
                    ins.then_inc(ring_t.full(key), 1)

            def values(i, q):
                pe.wait_ge(y_emptied, T * i + q)
                if q == 0:
                    for n in range(2):
                        key = ("v", n)
                        pe.wait_ge(ring_s.emptied(key), ring_s.uses(key, i) + 1)
                for n, js in enumerate(blocks(q)):
                    key = ("p", q, n)
                    pe.wait_ge(ring_t.emptied(key), ring_t.uses(key, i) + 1)
                    for j in js:
                        ins = pe.matmul(y_bank[:, 0:D], prob_t[:, q % 2, j, :], v[:, j, :],
                                        start=(j == 0), stop=(j == q))
                ins.then_inc(y_full, 1)

            def turn_y(i, q):
                key = ("y", q)
                pe.wait_ge(ring_t.emptied(key), ring_t.uses(key, i))
                pe.wait_ge(y_emptied, T * i + q + 1)
                for k in range(KD):
                    ins = pe.transpose(ring_t.view(key)[:, k * P:(k + 1) * P], y[:, q % 2, k * P:(k + 1) * P],
                                       ident[:, :])
                ins.then_inc(ring_t.full(key), 1)

            def output(i, q):
                key = ("y", q)
                pe.wait_ge(ring_t.emptied(key), ring_t.uses(key, i) + 1)
                f.pe_out(pe, i, q, lambda k: yt[:, q % 2, k, :], lambda k: w_out[:, k, :])

            def step(i, s, route=None):
                if s < T:
                    scores_of(i, s)
                if 0 <= s - 1 < T:
                    turn_prob(i, s - 1)
                if route is not None:
                    if s > 4:
                        pe.wait_ge(f.out_added, T * i + s - 4)
                    f.pe_route_turn(pe, route, routed(s)[0])
                if 0 <= s - 2 < T:
                    values(i, s - 2)
                if route is not None:
                    f.pe_route_logits(pe, route, routed(s)[0])
                if 0 <= s - 3 < T:
                    turn_y(i, s - 3)
                if 0 <= s - 4 < T:
                    if route is not None:
                        pe.wait_ge(f.logits_taken, T * route + s + 1)
                    output(i, s - 4)
                if route is not None:
                    for t in routed(s)[1:]:
                        f.pe_route_turn(pe, route, t)
                        f.pe_route_logits(pe, route, t)

            def batch(i, before, ahead):
                if before:
                    step(i - 1, T)
                latents(i, 0)
                if before:
                    step(i - 1, T + 1)
                latents(i, 1)
                value_rows(i, 0)
                if before:
                    step(i - 1, T + 2)
                    step(i - 1, T + 3)
                value_rows(i, 1)
                for s in range(T):
                    step(i, s, i - 1 if before and routed(s) else None)
                if ahead:
                    for h in range(HALVES):
                        f.pe_turn(pe, ring_s, i + 1, h)
            for h in range(HALVES):
                f.pe_turn(pe, ring_s, 0, h)
            pe.wait_ge(w_ready, 1)
            batch(0, False, True)
            with pe.Fori(1, B - 1) as i:
                batch(i, True, True)
            batch(B - 1, True, False)
            for s in range(T, STEPS):
                step(B - 1, s)
            f.pe_last_route(pe)

        @block.vector
        def _(dve):
            f.dve_stats(dve, 0, range(T))
            f.dve_mean(dve, 0)
            dve.wait_ge(w_high_ready, 1)
            dve.tensor_tensor(w_low[:, :, :], raw[:, :, :], high(w_high[:, :, :]), ALU.subtract)\
                .then_inc(w_ready, 1)
            f.dve_norm(dve, 0, range(T))
            for h in range(HALVES):
                f.dve_turn(dve, ring_s, 0, h)

            def latents(i, h):
                key, cols = ("l", h), slice(h * BANK, (h + 1) * BANK)
                ps = ring_s.view(key)[:, 0:BANK]
                dve.wait_ge(ring_s.full(key), ring_s.uses(key, i) + 1)
                dve.wait_ge(lat_high_ready, 2 * (HALVES * i + h + 1))
                dve.tensor_tensor(lat_both[R:P, cols], ps[R:P], high(lat_high[R:P, cols]), ALU.subtract)
                dve.tensor_tensor(lat_low[:, cols], ps, high(lat_high[:, cols]), ALU.subtract)\
                    .then_inc(ring_s.emptied(key), 1)

            def v_rows(i, n):
                key = ("v", n)
                dve.wait_ge(ring_s.full(key), ring_s.uses(key, i) + 1)
                dve.tensor_tensor(v[:, 4 * n:4 * n + 4, :],
                                  ring_s.view(key).rearrange("p (t c) -> p t c", c=D),
                                  bias_v[:, :].unsqueeze(1).to_broadcast([P, 4, D]), ALU.add)\
                    .then_inc(ring_s.emptied(key), 1)

            def peaks(i, q):
                key, n = ("s", q), (q + 1) * P
                dve.wait_ge(ring_s.full(key), ring_s.uses(key, i) + 1)
                dve.tensor_reduce(peak[:, q:q + 1], ring_s.view(key)[:, 0:n], AX.X, ALU.max)\
                    .then_inc(peak_done, 1)
                dve.wait_ge(peak_done, T * i + q + 1)
                dve.tensor_scalar(shift[:, q:q + 1], peak[:, q:q + 1], -(R ** -0.5), None, ALU.mult)\
                    .then_inc(shift_done, 1)

            def prob_turned(i, q):
                for n, js in enumerate(blocks(q)):
                    if n % 2 == 1:
                        key = ("p", q, n)
                        dve.wait_ge(ring_t.full(key), ring_t.uses(key, i) + 1)
                        dve.tensor_copy(prob_t[:, q % 2, js[0]:js[-1] + 1, :],
                                        ring_t.view(key)[:, 0:len(js) * P].rearrange("p (j t) -> p j t", t=P))\
                            .then_inc(ring_t.emptied(key), 1)

            def y_rows(i, q):
                key = ("s", q)
                dve.wait_ge(ring_s.emptied(key), ring_s.uses(key, i) + 1)
                dve.reciprocal(share[:, q:q + 1], total[:, q:q + 1]).then_inc(share_done, 1)
                dve.wait_ge(share_done, T * i + q + 1)
                dve.wait_ge(y_full, T * i + q + 1)
                dve.tensor_scalar(y[:, q % 2, :], y_bank[:, 0:D], share[:, q:q + 1], None, ALU.mult)\
                    .then_inc(y_emptied, 1)

            def step(i, s, route=None):
                if 0 <= s - 1 < T:
                    prob_turned(i, s - 1)
                if 0 <= s - 2 < T:
                    y_rows(i, s - 2)
                if route is not None:
                    for t in routed(s):
                        f.dve_route_logits(dve, route, t)
                if 0 <= s - 4 < T:
                    f.dve_out(dve, i, s - 4)
                    f.dve_stats2(dve, i, s - 4)

            half = T // 2

            def batch(i, before, ahead):
                if before:
                    step(i - 1, T)
                latents(i, 0)
                if before:
                    step(i - 1, T + 1)
                latents(i, 1)
                v_rows(i, 0)
                if before:
                    step(i - 1, T + 2)
                    step(i - 1, T + 3)
                    f.dve_mean2(dve, i - 1)
                v_rows(i, 1)
                for s in range(T):
                    peaks(i, s)
                    step(i, s, i - 1 if before and routed(s) else None)
                    if before and s < 2:
                        f.dve_norm2(dve, i - 1, range(half * s, half * (s + 1)))
                    if ahead and s in (1, 2):
                        f.dve_stats(dve, i + 1, range(half * (s - 1), half * s))
                    if ahead and s == 3:
                        f.dve_mean(dve, i + 1)
                    if ahead and s in (5, 6):
                        f.dve_norm(dve, i + 1, range(half * (s - 5), half * (s - 4)))
                if before:
                    dve.wait_ge(f.logits_taken, T * i)
                    f.dve_softmax(dve, i - 1)
                if ahead:
                    for h in range(HALVES):
                        f.dve_turn(dve, ring_s, i + 1, h)
                if before:
                    f.dve_scores(dve, i - 1)
            batch(0, False, True)
            with dve.Fori(1, B - 1) as i:
                batch(i, True, True)
            batch(B - 1, True, False)
            for s in range(T, STEPS):
                step(B - 1, s)
            f.dve_mean2(dve, B - 1)
            f.dve_norm2(dve, B - 1, range(T))
            f.dve_last_route(dve)
            f.dve_softmax(dve, B - 1)
            f.dve_scores(dve, B - 1)


GROUPS = B * HALVES
PIECES = 6
FB = F // P
ROUNDS = CAP // 8


def experts(nc, tag, sem, x_in, xn_in, wg_t, wu_t, wd_t, sg_t, su_t, sd_t, acc, ident, scores, batch_start):
    with ExitStack() as ctx:
        def sb(name, shape, dt=F32):
            return ctx.enter_context(nc.sbuf_tensor(f"{tag}_{name}", shape, dt))

        def bank(name):
            return ctx.enter_context(nc.psum_tensor(f"{tag}_bank_{name}", [P, BANK], F32))

        raw = sb("raw", [P, PIECES, BANK])
        w_high = [sb(f"w_high{n}", [P, PIECES, BANK], F32R) for n in range(2)]
        w_low = [sb(f"w_low{n}", [P, PIECES, BANK], F32R) for n in range(2)]
        tok = sb("tok", [P, 2, TH, D])
        xt_high = sb("xt_high", [P, 2, KD, BANK], F32R)
        xt_low = sb("xt_low", [P, 2, KD, BANK], F32R)
        act_out = sb("act_out", [P, 2, BANK])
        h = sb("h", [P, 2, BANK])
        h_high = sb("h_high", [P, 2, FB, BANK], F32R)
        h_low = sb("h_low", [P, 2, FB, BANK], F32R)
        res = sb("res", [P, 2, TH, D])
        by_expert = sb("by_expert", [P, S])
        top8 = sb("top8", [P, 8])
        at8 = sb("at8", [P, 8], U32)
        top = sb("top", [P, CAP])
        at = sb("at", [P, CAP])
        start = sb("start", [P, 1])
        weight = sb("weight", [P, B, E])
        token = sb("token", [P, B, E], U32)
        take_from = sb("take_from", [P, 2, TH], U32)
        add_to = sb("add_to", [P, 2, TH], U32)

        g_bank = [bank(f"g{n}") for n in range(2)]
        u_bank = [bank(f"u{n}") for n in range(2)]
        t_bank = [bank(f"t{n}") for n in range(2)]
        o_bank = [bank(f"o{n}") for n in range(2)]

        passed = sem("passed")
        w_loaded = [sem(f"w_loaded{n}") for n in range(3)]
        w_high_done, w_low_done = sem("w_high_done"), sem("w_low_done")
        tok_loaded = [sem(f"tok_loaded{n}") for n in range(2)]
        tok_gathered = [ctx.enter_context(nc.semaphore(f"{tag}_tok_gathered{n}")) for n in range(2)]
        res_loaded = [sem(f"res_loaded{n}") for n in range(2)]
        stored = [sem(f"stored{n}") for n in range(2)]
        scattered = [ctx.enter_context(nc.semaphore(f"{tag}_scattered{n}")) for n in range(2)]
        take_set = [sem(f"take_set{n}") for n in range(2)]
        add_set = [sem(f"add_set{n}") for n in range(2)]
        turn_full = [sem(f"turn_full{n}") for n in range(KD)]
        turned = [sem(f"turned{n}") for n in range(KD)]
        xt_high_done = sem("xt_high_done")
        g_full = [sem(f"g_full{n}") for n in range(2)]
        gelu_done = [sem(f"gelu_done{n}") for n in range(2)]
        u_full = [sem(f"u_full{n}") for n in range(2)]
        h_done = [sem(f"h_done{n}") for n in range(2)]
        h_high_done, h_low_done = sem("h_high_done"), sem("h_low_done")
        o_full = [sem(f"o_full{n}") for n in range(2)]
        o_taken = [sem(f"o_taken{n}") for n in range(2)]
        start_loaded = sem("start_loaded")
        by_expert_full, by_expert_done = sem("by_expert_full"), sem("by_expert_done")
        max_done, at_done, kept, replaced = sem("max_done"), sem("at_done"), sem("kept"), sem("replaced")
        at_ready = sem("at_ready")

        def gate(w, k, f):
            return w[:, k, f * P:(f + 1) * P]

        def up(w, k, f):
            return w[:, KD + k, f * P:(f + 1) * P]

        def down(w, f):
            return w[:, 2 * KD + f // 2, (f % 2) * D:(f % 2 + 1) * D]

        def piece_low(eng, w, slot, piece):
            eng.wait_ge(w_high_done, PIECES * w + piece + 1)
            eng.tensor_tensor(w_low[slot][:, piece, :], raw[:, piece, :], high(w_high[slot][:, piece, :]),
                              ALU.subtract).then_inc(w_low_done, 1)

        block = ctx.enter_context(nc.Block())

        @block.sync
        def _(sp):
            x_rows = x_in.rearrange("b (h t p) d -> (b h) p t d", p=P, t=TH)
            xn_rows = xn_in.rearrange("(n t p) d -> n p t d", p=P, t=TH)
            acc_rows = acc.rearrange("(n t p) d -> n p t d", p=P, t=TH)

            def group(rows, n):
                return rows[bass.ds(n, 1)].rearrange("a p t d -> p (a t) d")

            def weights(g, u, d):
                for n, w in enumerate((g, u)):
                    sp.dma_start(raw[:, KD * n:KD * (n + 1), :],
                                 w.rearrange("(k p) f -> p k f", p=P)).then_inc(w_loaded[n], 16)
                sp.dma_start(raw[:, 2 * KD:PIECES, :].rearrange("p k (c d) -> p (k c) d", d=D),
                             d.rearrange("(k p) d -> p k d", p=P)).then_inc(w_loaded[2], 16)

            def load_tok(n, p):
                sp.dma_start(tok[:, p, :, :], group(xn_rows, n)).then_inc(tok_loaded[p], 16)

            def load_res(n, p):
                sp.dma_start(res[:, p, :, :], group(x_rows, n)).then_inc(res_loaded[p], 16)

            def store(n, p, b):
                for c in range(2):
                    sp.wait_ge(o_taken[c], n + 1)
                sp.sem_inc(passed, 1)
                sp.dma_start(group(acc_rows, n), res[:, p, :, :]).then_inc(stored[p], 16)
                sp.wait_ge(stored[p], 16 * (b + 1))
                sp.sem_inc(passed, 1)

            def expert(e):
                sp.wait_ge(w_high_done, PIECES * (e + 1))
                sp.wait_ge(w_low_done, PIECES * (e + 1))
                sp.sem_inc(passed, 1)
                weights(wg_t[bass.ds(e, 1)].rearrange("a d f -> (a d) f"),
                        wu_t[bass.ds(e, 1)].rearrange("a d f -> (a d) f"),
                        wd_t[bass.ds(e, 1)].rearrange("a f d -> (a f) d"))

            load_tok(0, 0)
            weights(sg_t, su_t, sd_t)
            sp.dma_start(start[:, :], batch_start).then_inc(start_loaded, 16)
            load_res(0, 0)
            load_tok(1, 1)
            load_res(1, 1)
            expert(0)
            with sp.Fori(1, B) as b:
                for p in range(2):
                    for k in range(KD):
                        sp.wait_ge(turn_full[k], 2 * b + p - 1)
                        sp.sem_inc(passed, 1)
                    sp.wait_ge(tok_loaded[p], 16 * b)
                    sp.sem_inc(passed, 1)
                    load_tok(2 * b + p, p)
                    store(2 * b + p - 2, p, b - 1)
                    load_res(2 * b + p, p)
            expert(1)
            for p in range(2):
                store(GROUPS - 2 + p, p, B - 1)
            with sp.Fori(2, E) as e:
                expert(e)

        @block.gpsimd
        def _(pool):
            def gather(n, e, p):
                for k in range(KD):
                    pool.wait_ge(turn_full[k], n - 1)
                pool.sem_inc(passed, 1)
                pool.tensor_copy(take_from[:, p, :].unsqueeze(2), token[:, TH * p:TH * p + TH, bass.ds(e, 1)])\
                    .then_inc(take_set[p], 1)
                pool.wait_ge(take_set[p], e + 1)
                pool.sem_inc(passed, 1)
                for t in range(TH):
                    pool.indirect_dma_start(
                        out=tok[:, p, t, :], out_offset=None, in_=xn_in,
                        in_offset=bass.IndirectOffsetOnAxis(ap=take_from[:, p, t:t + 1], axis=0))\
                        .then_inc(tok_gathered[p], 16)

            def scatter(n, e, p):
                for half in range(2):
                    pool.wait_ge(stored[half], 16 * B)
                for c in range(2):
                    pool.wait_ge(o_taken[c], n + 1)
                pool.sem_inc(passed, 1)
                pool.tensor_copy(add_to[:, p, :].unsqueeze(2), token[:, TH * p:TH * p + TH, bass.ds(e, 1)])\
                    .then_inc(add_set[p], 1)
                pool.wait_ge(add_set[p], e + 1)
                pool.sem_inc(passed, 1)
                for t in range(TH):
                    pool.indirect_dma_start(
                        out=acc, out_offset=bass.IndirectOffsetOnAxis(ap=add_to[:, p, t:t + 1], axis=0),
                        in_=res[:, p, t, :], in_offset=None, compute_op=ALU.add).then_inc(scattered[p], 16)

            pool.wait_ge(w_low_done, 2 * KD)
            for piece in range(2 * KD, PIECES):
                piece_low(pool, 0, 0, piece)
            for piece in range(PIECES):
                piece_low(pool, 1, 1, piece)
            pool.wait_ge(by_expert_done, 4)
            gather(GROUPS, 0, 0)
            gather(GROUPS + 1, 0, 1)
            def step(q, j, prepare):
                n, e, p = GROUPS + 4 * q + j, 2 * q + j // 2, j % 2
                if prepare or j < 2:
                    gather(n + 2, e + 1, p)
                    if p == 0:
                        for piece in range(PIECES // 2):
                            piece_low(pool, e + 2, j // 2, piece)
                scatter(n, e, p)

            with pool.Fori(0, E // 2 - 1) as q:
                for j in range(4):
                    step(q, j, True)
            for j in range(4):
                step(E // 2 - 1, j, False)
            for p in range(2):
                pool.wait_ge(scattered[p], 16 * TH * E)

        @block.scalar
        def _(act):
            def piece_high(w, slot, piece):
                act.wait_ge(w_loaded[piece // KD], 16 * (w + 1))
                act.activation(w_high[slot][:, piece, :], raw[:, piece, :], ACT.Copy).then_inc(w_high_done, 1)

            def token_high(n, p):
                for k in range(KD):
                    act.wait_ge(turn_full[k], n + 1)
                    act.activation(xt_high[:, p, k, :], t_bank[k][:, :], ACT.Copy).then_inc(xt_high_done, 1)

            def gelu(n, f):
                act.wait_ge(g_full[f % 2], 2 * n + f // 2 + 1)
                act.wait_ge(h_done[f % 2], 2 * n + f // 2)
                act.activation(act_out[:, f % 2, :], g_bank[f % 2][:, :], ACT.Gelu).then_inc(gelu_done[f % 2], 1)

            def hidden_high(n, p, f):
                act.wait_ge(h_done[f % 2], 2 * n + f // 2 + 1)
                act.activation(h_high[:, p, f, :], h[:, f % 2, :], ACT.Copy).then_inc(h_high_done, 1)

            def step(n, p, turn, split=None):
                def third(c):
                    if split is not None:
                        w, slot = split
                        piece_high(w, slot, 3 * p + c)

                gelu(n, 0)
                gelu(n, 1)
                hidden_high(n, p, 0)
                third(0)
                if turn:
                    token_high(n + 1, 1 - p)
                gelu(n, 2)
                hidden_high(n, p, 1)
                third(1)
                third(2)
                gelu(n, 3)
                hidden_high(n, p, 2)
                hidden_high(n, p, 3)

            token_high(0, 0)
            for piece in range(PIECES):
                piece_high(0, 0, piece)
            for p in range(2):
                step(p, p, True, (1, 1))
            with act.Fori(1, B) as b:
                for p in range(2):
                    step(2 * b + p, p, True)
            with act.Fori(0, E // 2 - 1) as q:
                for j in range(4):
                    step(GROUPS + 4 * q + j, j % 2, True, (2 * q + j // 2 + 2, j // 2))
            for j in range(4):
                q = E // 2 - 1
                step(GROUPS + 4 * q + j, j % 2, j < 3, (2 * q + 2, 0) if j < 2 else None)

        @block.tensor
        def _(pe):
            for t in range(T):
                ins = pe.transpose(o_bank[t // TH][:, (t % TH) * P:(t % TH + 1) * P],
                                   scores[:, t, :, :].rearrange("p b e -> p (b e)"), ident[:, :])
            ins.then_inc(by_expert_full, 1)

            def turn(n, p, loaded, value):
                pe.wait_ge(loaded[p], value)
                for k in range(KD):
                    pe.wait_ge(turned[k], n)
                    for t in range(TH):
                        ins = pe.transpose(t_bank[k][:, t * P:(t + 1) * P], tok[:, p, t, k * P:(k + 1) * P],
                                           ident[:, :])
                    ins.then_inc(turn_full[k], 1)

            def hidden(n, p, slot, f):
                for banks, full, read, part in ((g_bank, g_full, gelu_done, gate), (u_bank, u_full, h_done, up)):
                    pe.wait_ge(read[f % 2], 2 * n + f // 2)
                    three_products(pe, banks[f % 2][:, :],
                                   lambda k: part(w_high[slot], k, f), lambda k: part(w_low[slot], k, f),
                                   lambda k: xt_high[:, p, k, :], lambda k: xt_low[:, p, k, :],
                                   range(KD)).then_inc(full[f % 2], 1)

            def output(n, p, slot):
                pe.wait_ge(h_low_done, FB * (n + 1))
                for c in range(2):
                    pe.wait_ge(o_taken[c], n)
                    for t in range(2):
                        rows = slice((2 * c + t) * P, (2 * c + t + 1) * P)
                        ins = three_products(pe, o_bank[c][:, t * D:(t + 1) * D],
                                             lambda f: h_high[:, p, f, rows], lambda f: h_low[:, p, f, rows],
                                             lambda f: down(w_high[slot], f), lambda f: down(w_low[slot], f),
                                             range(FB))
                    ins.then_inc(o_full[c], 1)

            def step(n, p, slot, before, after, choice=False):
                for k in range(KD):
                    pe.wait_ge(turned[k], n + 1)
                hidden(n, p, slot, 0)
                if before is not None:
                    output(n - 1, 1 - p, before)
                hidden(n, p, slot, 1)
                if choice:
                    pe.wait_ge(by_expert_done, 4)
                if after is not None:
                    turn(n + 1, 1 - p, *after)
                hidden(n, p, slot, 2)
                hidden(n, p, slot, 3)

            def shared(b, p, first=False, last=False, choice=False):
                after = (tok_gathered, 16 * TH) if last else (tok_loaded, 16 * (b + p + 1))
                step(2 * b + p, p, 0, None if first else 0, after, choice)

            turn(0, 0, tok_loaded, 16)
            pe.wait_ge(w_low_done, 2 * KD)
            pe.wait_ge(by_expert_done, 2)
            shared(0, 0, first=True)
            pe.wait_ge(w_low_done, PIECES)
            shared(0, 1)
            with pe.Fori(1, B - 2) as b:
                for p in range(2):
                    shared(b, p)
            for p in range(2):
                shared(B - 2, p)
            pe.wait_ge(turned[0], GROUPS - 1)
            pe.wait_ge(at_ready, 1)
            pe.transpose(t_bank[0][:, 0:P], top[:, :], ident[:, :])
            pe.transpose(t_bank[0][:, P:2 * P], at[:, :], ident[:, :]).then_inc(by_expert_full, 1)
            shared(B - 1, 0, choice=True)
            shared(B - 1, 1, last=True)

            def routed(q, j, last=False):
                n, e, p = GROUPS + 4 * q + j, 2 * q + j // 2, j % 2
                if p == 0:
                    pe.wait_ge(w_low_done, PIECES * (e + 2))
                after = None if last else (tok_gathered, 16 * TH * (e + 1 + p))
                step(n, p, 1 - j // 2, (0, 1, 1, 0)[j], after)

            with pe.Fori(0, E // 2 - 1) as q:
                for j in range(4):
                    routed(q, j)
            for j in range(4):
                routed(E // 2 - 1, j, last=j == 3)
            output(GROUPS + 2 * E - 1, 1, 0)

        @block.vector
        def _(dve):
            for c in range(2):
                dve.wait_ge(by_expert_full, 1)
                dve.tensor_copy(by_expert[:, c * BANK:(c + 1) * BANK], o_bank[c][:, :]).then_inc(by_expert_done, 1)
            dve.wait_ge(by_expert_done, 2)

            def token_low(n, p):
                for k in range(KD):
                    dve.wait_ge(xt_high_done, KD * n + k + 1)
                    dve.tensor_tensor(xt_low[:, p, k, :], t_bank[k][:, :], high(xt_high[:, p, k, :]),
                                      ALU.subtract).then_inc(turned[k], 1)

            def hidden(n, f):
                dve.wait_ge(gelu_done[f % 2], 2 * n + f // 2 + 1)
                dve.wait_ge(u_full[f % 2], 2 * n + f // 2 + 1)
                if not (isinstance(n, int) and FB * n + f < 2):
                    dve.wait_ge(h_low_done, FB * n + f - 1)
                dve.tensor_tensor(h[:, f % 2, :], u_bank[f % 2][:, :], act_out[:, f % 2, :], ALU.mult)\
                    .then_inc(h_done[f % 2], 1)

            def hidden_low(n, p, f):
                dve.wait_ge(h_high_done, FB * n + f + 1)
                dve.tensor_tensor(h_low[:, p, f, :], h[:, f % 2, :], high(h_high[:, p, f, :]), ALU.subtract)\
                    .then_inc(h_low_done, 1)

            def add_residual(n, p, b):
                dve.wait_ge(res_loaded[p], 16 * (b + 1))
                for c in range(2):
                    dve.wait_ge(o_full[c], n + 1)
                    rows = res[:, p, 2 * c:2 * c + 2, :]
                    dve.tensor_tensor(rows, o_bank[c][:, :].rearrange("p (t d) -> p t d", d=D), rows, ALU.add)\
                        .then_inc(o_taken[c], 1)

            def weigh(n, p, e):
                dve.wait_ge(stored[p], 16 * B)
                dve.wait_ge(scattered[p], 16 * TH * e)
                for c in range(2):
                    dve.wait_ge(o_full[c], n + 1)
                    for t in range(2):
                        ins = dve.tensor_scalar(res[:, p, 2 * c + t, :], o_bank[c][:, t * D:(t + 1) * D],
                                                weight[:, TH * p + 2 * c + t, bass.ds(e, 1)], None, ALU.mult)
                    ins.then_inc(o_taken[c], 1)

            def largest(r):
                dve.wait_ge(replaced, r)
                dve.sem_inc(passed, 1)
                dve.max(top8[:, :], by_expert[:, :]).then_inc(max_done, 1)

            def places(r):
                dve.wait_ge(max_done, r + 1)
                dve.sem_inc(passed, 1)
                dve.max_index(at8[:, :], top8[:, :], by_expert[:, :]).then_inc(at_done, 1)

            def take(r):
                dve.wait_ge(at_done, r + 1)
                dve.sem_inc(passed, 1)
                dve.match_replace(by_expert[:, :], top8[:, :], by_expert[:, :], -1.0).then_inc(replaced, 1)
                dve.tensor_copy(top[:, bass.ds(8 * r, 8)], top8[:, :]).then_inc(kept, 1)
                dve.tensor_copy(at[:, bass.ds(8 * r, 8)], at8[:, :]).then_inc(kept, 1)
                dve.wait_ge(kept, 2 * r + 2)

            def step(n, p, finish, turn=True, rounds=(), split=None):
                def third(c):
                    if split is not None:
                        w, slot = split
                        piece_low(dve, w, slot, PIECES // 2 + c)

                hidden(n, 0)
                if finish is not None:
                    finish[0](n - 1, 1 - p, finish[1])
                if rounds:
                    largest(rounds[0])
                hidden(n, 1)
                hidden_low(n, p, 0)
                third(0)
                if turn:
                    token_low(n + 1, 1 - p)
                if rounds:
                    places(rounds[0])
                hidden(n, 2)
                hidden_low(n, p, 1)
                third(1)
                third(2)
                if rounds:
                    take(rounds[0])
                hidden(n, 3)
                hidden_low(n, p, 2)
                hidden_low(n, p, 3)
                for r in rounds[1:]:
                    largest(r)
                    places(r)
                    take(r)

            def shared(b, p, rounds=(), first=False):
                step(2 * b + p, p, None if first else (add_residual, b - 1 + p), rounds=rounds)

            token_low(0, 0)
            for piece in range(2 * KD):
                piece_low(dve, 0, 0, piece)
            shared(0, 0, (0,), first=True)
            shared(0, 1, (1, 2))
            with dve.Fori(1, ROUNDS // 3) as b:
                shared(b, 0, (3 * b,))
                shared(b, 1, (3 * b + 1, 3 * b + 2))
            shared(5, 0, (ROUNDS - 1,))
            dve.wait_ge(start_loaded, 16)
            dve.tensor_scalar(at[:, :], at[:, :], start[:, :], None, ALU.add).then_inc(at_ready, 1)
            shared(5, 1)
            shared(6, 0)
            shared(6, 1)
            dve.wait_ge(by_expert_full, 2)
            dve.tensor_copy(weight[:, :, :].rearrange("p b e -> p (b e)"), t_bank[0][:, 0:P]).then_inc(by_expert_done, 1)
            dve.tensor_copy(token[:, :, :].rearrange("p b e -> p (b e)"), t_bank[0][:, P:2 * P])\
                .then_inc(by_expert_done, 1)
            shared(7, 0)
            shared(7, 1)
            def routed(q, j, first=False, last=False):
                n, e, p = GROUPS + 4 * q + j, 2 * q + j // 2, j % 2
                finish = (add_residual, B - 1) if first else (weigh, e - 1 + p)
                prepare = p == 1 and not (isinstance(q, int) and q == E // 2 - 1 and j == 3)
                step(n, p, finish, turn=not last, split=(e + 2, j // 2) if prepare else None)

            for j in range(4):
                routed(0, j, first=j == 0)
            with dve.Fori(1, E // 2 - 1) as q:
                for j in range(4):
                    routed(q, j)
            for j in range(4):
                routed(E // 2 - 1, j, last=j == 3)
            weigh(GROUPS + 2 * E - 1, 1, E - 1)


H, HD = 4, 64
HALF = HD // 2
Q4 = HALF // 2
BASE_MIN, BASE_SPAN = 8300.0, 3400.0
PI = 3.1415925


def attention_b(nc, x_in, w_q, w_k, w_v, b_q, b_k, b_v, w_o, b_o, freq, position, exponent,
                x_out, xn_out, ident, gate, scores):
    with ExitStack() as ctx:
        f = Frame(nc, ctx, "b", x_in, x_out, xn_out, ident, gate, scores, one_norm=True)
        sb, sem = f.sb, f.sem
        QK = 2 * H * HD
        w_high = sb("w_high", [P, KD, QK + D], F32R)
        w_low = sb("w_low", [P, KD, QK + D], F32R)
        w_out = sb("w_out", [P, KD, D])
        bias_in = sb("bias_in", [P, QK + D])
        cos = sb("cos", [P, T, Q4])
        sin = sb("sin", [P, T, Q4])
        qk = sb("qk", [P, T, QK])
        v = sb("v", [P, T, D])
        q_high = sb("q_high", [P, H, S], F32R)
        q_low = sb("q_low", [P, H, S], F32R)
        k_both = sb("k_both", [P, H, S], F32R)
        UNITS, STEPS_U = 4, 8
        G = UNITS * STEPS_U
        LAST = G + 10
        peak = sb("row_peak", [P, G])
        shift = sb("row_shift", [P, G])
        total = sb("row_total", [P, G])
        share = sb("row_share", [P, G])
        prob = sb("prob", [P, 2, S])
        turn_t = [prob[:, n // 2, (n % 2) * BANK:(n % 2 + 1) * BANK].rearrange("p (t h e) -> p t h e", t=TH, e=Q4)
                  for n in range(4)]
        prob_t = [[sb("prob_t00", [P, T, BANK]), sb("prob_t01", [P, T, BANK])], [sb("prob_t10", [P, T, BANK]), qk]]
        y_sum = sb("y_sum", [P, BANK])
        y_rows = sb("y_rows", [P, TH, P])
        yt = sb("yt", [P, 2, BANK])

        def bank(name, n=1):
            return ctx.enter_context(nc.psum_tensor(f"b_bank_{name}", [P, n * BANK], F32))

        s_banks = [bank(f"s{n}", 2) for n in range(2)]
        t_banks = [bank(f"t{n}") for n in range(2)]
        y_bank = bank("y")
        beside_bank = bank("beside")
        f.last_route(s_banks, prob[:, :, :],
                     [sem(f"last_{name}") for name in ("turn_full", "turned", "logits_full", "logits_taken")])

        def step_of(g):
            u = g // STEPS_U
            return u, u // 2, u % 2, (g % STEPS_U) // TH, g % TH

        def turns_prob(g):
            return g - 1 if 0 <= g - 1 < G else None

        def sums_values(g):
            return g - 10 if 0 <= g - 10 < G else None

        SOFTMAX = 27

        def stats_tiles(g):
            return range(g - 12, g - 10) if g in range(12, 12 + T, 2) else None
        MEAN = 13 + T

        def norm_tiles(g):
            return range(2 * (g - G + 5), 2 * (g - G + 6)) if G - 5 <= g < G - 5 + T // 2 else None

        def turns_x(g):
            return {G: 0, G + 2: 1}.get(g)

        parts_order = [("k", 0, 0), ("q", 0, 0), ("k", 0, 1), ("k", 1, 0), ("k", 1, 1), ("q", 1, 0), ("q", 0, 1),
                       ("q", 1, 1)]
        parts_first = parts_order[:3]

        beside = {2 * n: ("parts", *parts_order[3 + n]) for n in range(5)}
        beside.update({9 + 2 * t + (t > 4): ("route turn", t) for t in range(6)})
        beside.update({10 + 2 * t + (t > 4): ("logits", t) for t in range(6)})
        beside.update({23: ("route turn", 6), 24: ("logits", 6), 25: ("route turn", 7), 26: ("logits", 7)})
        beside.update({19 + STEPS_U * u: ("back", u) for u in range(UNITS - 1)})
        beside.update({22: ("forth", 0), 29: ("forth", 1), 37: ("forth", 2)})
        beside.update({31 + t: ("out", t) for t in range(TH)})
        assert len(beside) == 5 + 2 * T + 2 * (UNITS - 1) + TH

        t_keys = [("parts", *part) for part in parts_first[:2]]
        for g in range(LAST):
            if turns_prob(g) is not None:
                t_keys += [("p", turns_prob(g), n) for n in range(2)]
        t_keys += [("back", UNITS - 1), ("forth", UNITS - 1)]
        ring_t = Ring(sem, "t", [b[:, :] for b in t_banks], t_keys)
        beside_keys = [("parts", *parts_first[2])] + [beside[g] for g in sorted(beside)]
        ring_b = Ring(sem, "beside", [beside_bank[:, :]], beside_keys,
                      not_first=[key for key in beside_keys if key[0] in ("route turn", "logits")])

        def ring_of(key):
            return ring_b if key in ring_b.at else ring_t

        ahead_keys = [("x", h) for h in range(HALVES)] + [("qk", n) for n in range(T // 2)]
        ring_s = Ring(sem, "s", [b[:, :] for b in s_banks],
                      [("v", n) for n in range(2)] + [("s", g) for g in range(G)] + ahead_keys
                      + [("out", n) for n in range(2)], before=ahead_keys)
        y_full, y_emptied = sem("y_full"), sem("y_emptied")
        w_loaded, w_high_ready, w_ready = sem("w_loaded"), sem("w_high_ready"), sem("w_ready")
        angle_step, tables_ready = sem("angle_step"), sem("tables_ready")
        rope_step = sem("rope_step")
        part_high = sem("part_high")
        parts_copied = [[sem(f"parts_copied{pair}{c}") for c in range(HALVES)] for pair in range(2)]
        peak_done, shift_done, share_done = sem("row_peak_done"), sem("row_shift_done"), sem("row_share_done")

        raw = qk[:, :, :].rearrange("p t c -> p (t c)")[:, 0:KD * (QK + D)].rearrange("p (k c) -> p k c", k=KD)
        freq_b = peak[:, 0:1]
        base = [shift[:, n:n + 1] for n in range(4)]
        position_b = total[:, 0:T]
        exponent_b = share[:, 0:Q4]
        inverse = share[:, Q4:2 * Q4]
        angle = [turn_t[n][:, 0, :, :] for n in range(4)]

        def halves(c):
            heads = qk[:, TH * c:TH * (c + 1), :].rearrange("p t (h e) -> p t h e", e=HD)
            return heads[:, :, :, HALF:HALF + Q4], heads[:, :, :, HALF + Q4:HD]

        def table(a, c):
            return a[:, TH * c:TH * (c + 1), :].unsqueeze(2).to_broadcast([P, TH, 2 * H, Q4])

        def rope_products(eng, i, c, n, tables):
            for m in (2 * c, 2 * c + 1):
                key = ("qk", m)
                eng.wait_ge(ring_s.emptied(key), ring_s.uses_ahead(key, i) + 1)
            done = 6 * (2 * i + c)
            if not (isinstance(i, int) and done == 0):
                eng.wait_ge(rope_step, done)
            for m in range(2):
                eng.tensor_tensor(turn_t[2 * n + m][:, :, :, :], halves(c)[m], table(tables[m], c), ALU.mult)\
                    .then_inc(rope_step, 1)

        def rope_sum(eng, i, c, n, op):
            eng.wait_ge(rope_step, 6 * (2 * i + c) + 4)
            eng.tensor_tensor(halves(c)[n], turn_t[2 * n][:, :, :, :], turn_t[2 * n + 1][:, :, :, :], op)\
                .then_inc(rope_step, 1)

        block = ctx.enter_context(nc.Block())

        @block.sync
        def _(sp):
            f.sp_load(sp, 0)
            for n, w in enumerate((w_q, w_k, w_v)):
                sp.dma_start(raw[:, :, n * D:(n + 1) * D], w.rearrange("(k p) c -> p k c", p=P)).then_inc(w_loaded, 16)
            for n, b in enumerate((b_q, b_k, b_v)):
                sp.dma_start(bias_in[:, n * D:(n + 1) * D], spread(b)).then_inc(w_loaded, 16)
            sp.dma_start(w_out[:, :, :], w_o.rearrange("(k p) c -> p k c", p=P)).then_inc(w_loaded, 16)
            sp.dma_start(f.bias_out[:, :], spread(b_o)).then_inc(w_loaded, 16)
            sp.dma_start(freq_b, spread(freq)).then_inc(w_loaded, 16)
            sp.dma_start(position_b, position).then_inc(w_loaded, 16)
            sp.dma_start(exponent_b, exponent).then_inc(w_loaded, 16)

            def copy_parts(i):
                for c in range(HALVES):
                    cols = slice(c * BANK, (c + 1) * BANK)
                    for pair in range(2):
                        key = ("parts", "q", pair, c)
                        sp.wait_ge(ring_of(key).emptied(key), ring_of(key).uses(key, i) + 1)
                        for part in (q_high, q_low):
                            for h, own, other in ((2 * pair, slice(0, HD), slice(HD, P)),
                                                  (2 * pair + 1, slice(HD, P), slice(0, HD))):
                                sp.dma_start(high(part[other, h, cols]), high(part[own, h, cols]))\
                                    .then_inc(parts_copied[pair][c], 16)

            f.sp_all(sp, copy_parts)

        LOADS = 11 * 16

        @block.gpsimd
        def _(pool):
            pool.memset(f.minus_half[:, :], -0.5).then_inc(f.half_set, 1)
            pool.wait_ge(f.half_set, 1)
            f.pool_rstd(pool, 0)
            pool.wait_ge(w_loaded, LOADS)
            pool.wait_ge(angle_step, 4)
            pool.tensor_tensor(inverse, base[3].to_broadcast([P, Q4]), exponent_b, ALU.pow).then_inc(angle_step, 1)
            pool.wait_ge(tables_ready, 2)

            def rotate(i):
                for c in range(HALVES):
                    rope_products(pool, i, c, 1, (sin, cos))
                    rope_sum(pool, i, c, 1, ALU.add)

            def ahead(i):
                f.pool_rstd(pool, i)
                f.pool_bias(pool, i)
            rotate(0)
            f.pool_bias(pool, 0)
            ahead(1)
            with pool.Fori(1, B - 1) as i:
                rotate(i)
                f.pool_rstd2(pool, i - 1)
                f.pool_norm2(pool, i - 1)
                ahead(i + 1)
            rotate(B - 1)
            f.pool_rstd2(pool, B - 2)
            f.pool_norm2(pool, B - 2)
            f.pool_rstd2(pool, B - 1)

        @block.scalar
        def _(act):
            act.wait_ge(w_loaded, LOADS)
            act.activation(base[0], freq_b, ACT.Exp, scale=-1.0).then_inc(angle_step, 1)
            act.activation(w_high[:, :, :], raw, ACT.Copy).then_inc(w_high_ready, 1)
            for h in range(HALVES):
                f.act_turn(act, ring_s, 0, h)
            act.wait_ge(angle_step, 9)
            act.activation(angle[2], angle[1], ACT.Sin).then_inc(angle_step, 1)
            act.activation(angle[3], angle[0], ACT.Sin).then_inc(angle_step, 1)

            def parts(i, kind, pair, c):
                to = q_high if kind == "q" else k_both
                cols = slice(c * BANK, (c + 1) * BANK)
                key = ("parts", kind, pair, c)
                act.wait_ge(ring_of(key).full(key), ring_of(key).uses(key, i) + 1)
                for hh in range(2):
                    own = slice(hh * HD, (hh + 1) * HD)
                    act.activation(to[own, 2 * pair + hh, cols], ring_of(key).view(key)[own], ACT.Copy).then_inc(part_high, 1)

            def exps(i, g):
                key = ("s", g)
                act.wait_ge(shift_done, G * i + g + 1)
                if g >= 2:
                    last = ("p", g - 2, 1)
                    act.wait_ge(ring_t.full(last), ring_t.uses(last, i) + 1)
                act.activation(prob[:, g % 2, :], ring_s.view(key), ACT.Exp, bias=shift[:, g:g + 1],
                               scale=HD ** -0.5, accum_out=total[:, g:g + 1]).then_inc(ring_s.emptied(key), 1)

            def prob_turned(i, g):
                u, _, _, hh, t = step_of(g)
                key = ("p", g, 0)
                act.wait_ge(ring_t.full(key), ring_t.uses(key, i) + 1)
                act.activation(prob_t[u % 2][hh][:, 0:4, t * P:(t + 1) * P],
                               ring_t.view(key).rearrange("p (j t) -> p j t", t=P), ACT.Copy)\
                    .then_inc(ring_t.emptied(key), 1)

            def take_sum(i, u):
                act.wait_ge(y_full, UNITS * i + u + 1)
                act.activation(y_sum[:, :], y_bank[:, :], ACT.Copy).then_inc(y_emptied, 1)

            def forth(i, u):
                key = ("forth", u)
                ring = ring_of(key)
                act.wait_ge(ring.full(key), ring.uses(key, i) + 1)
                act.activation(yt[:, u % 2, :], ring.view(key), ACT.Copy).then_inc(ring.emptied(key), 1)

            def route_turn(i, t):
                key = ("route turn", t)
                act.wait_ge(ring_b.full(key), ring_b.uses(key, i) + 1)
                act.activation(f.xn2t[:, :, :], ring_b.view(key)[:, 0:D].rearrange("p (k t) -> p k t", k=KD), ACT.Copy)\
                    .then_inc(ring_b.emptied(key), 1)

            def side(i, before, what, *at):
                if what == "parts":
                    parts(i, *at)
                elif what == "forth":
                    forth(i, *at)
                elif what == "route turn" and before:
                    route_turn(i, *at)

            def batch(i, before, ahead):
                if before:
                    forth(i - 1, UNITS - 1)
                for part in parts_first:
                    parts(i, *part)
                for g in range(LAST):
                    if sums_values(g) is not None and sums_values(g) % STEPS_U == STEPS_U - 1:
                        take_sum(i, sums_values(g) // STEPS_U)
                    if g in beside:
                        side(i, before, *beside[g])
                    if turns_prob(g) is not None:
                        prob_turned(i, turns_prob(g))
                    if g < G:
                        exps(i, g)
                    if before and g == SOFTMAX + 1:
                        f.act_softmax(act, i - 1)
                    if ahead and turns_x(g) is not None:
                        f.act_turn(act, ring_s, i + 1, turns_x(g))
            batch(0, False, True)
            with act.Fori(1, B - 1) as i:
                batch(i, True, True)
            batch(B - 1, True, False)
            forth(B - 1, UNITS - 1)
            f.act_last_route(act)
            f.act_softmax(act, B - 1)

        @block.tensor
        def _(pe):
            def projections(i, key, uses, first, c, e):
                if first % TH == 0:
                    f.pe_wait_turned(pe, ring_s, i, first // TH)
                pe.wait_ge(ring_s.emptied(key), uses(key, i))
                w = e - c
                for m in range(2 * BANK // w):
                    rows = slice((first + m) * P, (first + m + 1) * P)
                    ins = three_products(pe, ring_s.view(key)[:, m * w:(m + 1) * w],
                                         lambda k: f.xt_high[:, k, rows], lambda k: f.xt_low[:, k, rows],
                                         lambda k: w_high[:, k, c:e], lambda k: w_low[:, k, c:e], range(KD))
                ins.then_inc(ring_s.full(key), 1)

            def qk_rows(i, n):
                projections(i, ("qk", n), ring_s.uses_ahead, 2 * n, 0, QK)

            def value_rows(i, n):
                projections(i, ("v", n), ring_s.uses, TH * n, QK, QK + D)

            def turn_parts(i, kind, pair, c):
                pe.wait_ge(rope_step, 6 * (2 * i + c + 1))
                key = ("parts", kind, pair, c)
                ring = ring_of(key)
                pe.wait_ge(ring.emptied(key), ring.uses(key, i))
                for t in range(TH):
                    a = "qk".index(kind) * H * HD + pair * P
                    ins = pe.transpose(ring.view(key)[:, t * P:(t + 1) * P], qk[:, TH * c + t, a:a + P], ident[:, :])
                ins.then_inc(ring.full(key), 1)

            def scores_of(i, g):
                u, c, pair, hh, t = step_of(g)
                if g % STEPS_U == 0:
                    for part in (("k", pair, 0), ("k", pair, 1), ("q", pair, c)):
                        key = ("parts", *part)
                        pe.wait_ge(ring_of(key).emptied(key), ring_of(key).uses(key, i) + 1)
                    pe.wait_ge(parts_copied[pair][c], 64 * (i + 1))
                key, h = ("s", g), 2 * pair + hh
                rows = slice(c * BANK + t * P, c * BANK + (t + 1) * P)
                pe.wait_ge(ring_s.emptied(key), ring_s.uses(key, i))
                for m in range(0, S, BANK):
                    out = ring_s.view(key)[:, m:m + BANK]
                    pe.matmul(out, q_high[:, h, rows], k_both[:, h, m:m + BANK], start=True, stop=False)
                    ins = pe.matmul(out, q_low[:, h, rows], k_both[:, h, m:m + BANK], start=False, stop=True)
                ins.then_inc(ring_s.full(key), 1)

            def turn_prob(i, g):
                key = ("s", g)
                pe.wait_ge(ring_s.emptied(key), ring_s.uses(key, i) + 1)
                for n in range(2):
                    key = ("p", g, n)
                    pe.wait_ge(ring_t.emptied(key), ring_t.uses(key, i))
                    for j in range(4):
                        ins = pe.transpose(ring_t.view(key)[:, j * P:(j + 1) * P],
                                           prob[:, g % 2, (4 * n + j) * P:(4 * n + j + 1) * P], ident[:, :])
                    ins.then_inc(ring_t.full(key), 1)

            def values(i, m):
                u, j = m // STEPS_U, m % STEPS_U
                pair = u % 2
                if j == 0:
                    pe.wait_ge(y_emptied, UNITS * i + u)
                    for n in range(2):
                        key = ("p", STEPS_U * (u + 1) - 1, n)
                        pe.wait_ge(ring_t.emptied(key), ring_t.uses(key, i) + 1)
                for hh in range(2):
                    h = 2 * pair + hh
                    ins = pe.matmul(y_bank[hh * HD:(hh + 1) * HD, :], v[:, j, h * HD:(h + 1) * HD],
                                    prob_t[u % 2][hh][:, j, :], start=(j == 0), stop=(j == T - 1))
                if j == T - 1:
                    ins.then_inc(y_full, 1)

            def turn_back(i, u):
                key = ("back", u)
                ring = ring_of(key)
                pe.wait_ge(y_emptied, UNITS * i + u + 1)
                pe.wait_ge(ring.emptied(key), ring.uses(key, i))
                for t in range(TH):
                    ins = pe.transpose(ring.view(key)[:, t * P:(t + 1) * P], y_sum[:, t * P:(t + 1) * P], ident[:, :])
                ins.then_inc(ring.full(key), 1)

            def turn_forth(i, u):
                back, key = ("back", u), ("forth", u)
                ring = ring_of(key)
                pe.wait_ge(ring.emptied(back), ring.uses(back, i) + 1)
                pe.wait_ge(ring.emptied(key), ring.uses(key, i))
                for t in range(TH):
                    ins = pe.transpose(ring.view(key)[:, t * P:(t + 1) * P], y_rows[:, t, :], ident[:, :])
                ins.then_inc(ring.full(key), 1)

            def output(i, t):
                forth, key = ("forth", 1), ("out", t)
                pe.wait_ge(ring_b.emptied(forth), ring_b.uses(forth, i) + 1)
                f.pe_outs(pe, ring_b, i, key, (t,), lambda t, k: yt[:, k, t * P:(t + 1) * P], lambda k: w_out[:, k, :])

            def route_turn(i, t):
                key = ("route turn", t)
                pe.wait_ge(f.xn2_ready, T * (i - 1) + t + 1)
                pe.wait_ge(ring_b.emptied(key), ring_b.uses(key, i))
                for k in range(KD):
                    ins = pe.transpose(ring_b.view(key)[:, k * P:(k + 1) * P], f.xn2[:, t, k * P:(k + 1) * P],
                                       ident[:, :])
                ins.then_inc(ring_b.full(key), 1)

            def route_logits(i, t):
                key = ("logits", t)
                pe.wait_ge(ring_b.emptied(key), ring_b.uses(key, i))
                for k in range(KD):
                    ins = pe.matmul(ring_b.view(key)[:, 0:E], f.xn2t[:, k, :], gate[:, k, :], start=(k == 0),
                                    stop=(k == KD - 1))
                ins.then_inc(ring_b.full(key), 1)

            def side(i, before, what, *at):
                if what == "parts":
                    turn_parts(i, *at)
                elif what == "back":
                    turn_back(i, *at)
                elif what == "forth":
                    turn_forth(i, *at)
                elif what == "out":
                    output(i, *at)
                elif before:
                    (route_turn if what == "route turn" else route_logits)(i, *at)

            def last_outputs(i):
                forth = ("forth", UNITS - 1)
                pe.wait_ge(ring_t.emptied(forth), ring_t.uses(forth, i) + 1)
                for n in range(2):
                    f.pe_outs(pe, ring_s, i, ("out", n), (TH + 2 * n, TH + 2 * n + 1),
                              lambda t, k: yt[:, k, (t - TH) * P:(t - TH + 1) * P], lambda k: w_out[:, k, :])

            def batch(i, before, ahead):
                qk_rows(i, 0)
                if before:
                    turn_back(i - 1, UNITS - 1)
                qk_rows(i, 1)
                if before:
                    turn_forth(i - 1, UNITS - 1)
                qk_rows(i, 2)
                qk_rows(i, 3)
                if before:
                    last_outputs(i - 1)
                for part in parts_first[:2]:
                    turn_parts(i, *part)
                value_rows(i, 0)
                turn_parts(i, *parts_first[2])
                value_rows(i, 1)
                for g in range(LAST):
                    if g < G:
                        scores_of(i, g)
                    if sums_values(g) is not None:
                        values(i, sums_values(g))
                    if g in beside:
                        side(i, before, *beside[g])
                    if ahead and turns_x(g) is not None:
                        f.pe_turn(pe, ring_s, i + 1, turns_x(g))
                    if turns_prob(g) is not None:
                        turn_prob(i, turns_prob(g))
            for h in range(HALVES):
                f.pe_turn(pe, ring_s, 0, h)
            pe.wait_ge(w_ready, 1)
            batch(0, False, True)
            with pe.Fori(1, B - 1) as i:
                batch(i, True, True)
            batch(B - 1, True, False)
            turn_back(B - 1, UNITS - 1)
            turn_forth(B - 1, UNITS - 1)
            last_outputs(B - 1)
            f.pe_last_route(pe)

        @block.vector
        def _(dve):
            f.dve_stats(dve, 0, range(T))
            f.dve_mean(dve, 0)
            dve.wait_ge(angle_step, 1)
            dve.tensor_scalar(base[1], base[0], 1.0, None, ALU.add).then_inc(angle_step, 1)
            dve.wait_ge(angle_step, 2)
            dve.reciprocal(base[2], base[1]).then_inc(angle_step, 1)
            dve.wait_ge(angle_step, 3)
            dve.tensor_scalar(base[3], base[2], BASE_SPAN, BASE_MIN, ALU.mult, ALU.add).then_inc(angle_step, 1)
            dve.wait_ge(w_high_ready, 1)
            dve.tensor_tensor(w_low[:, :, :], raw, high(w_high[:, :, :]), ALU.subtract).then_inc(w_ready, 1)
            f.dve_norm(dve, 0, range(T))
            for h in range(HALVES):
                f.dve_turn(dve, ring_s, 0, h)
            dve.wait_ge(angle_step, 5)
            dve.tensor_tensor(angle[0], position_b.unsqueeze(2).to_broadcast([P, T, Q4]),
                              inverse.unsqueeze(1).to_broadcast([P, T, Q4]), ALU.mult).then_inc(angle_step, 1)
            dve.wait_ge(angle_step, 6)
            dve.tensor_scalar(angle[2], angle[0], 2 * 3.141592653589793 / (S - 1), None, ALU.mult)\
                .then_inc(angle_step, 1)
            dve.wait_ge(angle_step, 7)
            dve.tensor_scalar(angle[1], angle[2], 3.141592653589793, PI, ALU.subtract, ALU.min).then_inc(angle_step, 1)
            dve.tensor_scalar(angle[0], angle[2], 0.5, PI, ALU.mult, ALU.min).then_inc(angle_step, 1)
            dve.wait_ge(angle_step, 11)
            dve.tensor_scalar(sin[:, :, :], angle[2], -1.0, None, ALU.mult).then_inc(tables_ready, 1)
            dve.tensor_tensor(angle[1], angle[3], angle[3], ALU.mult).then_inc(angle_step, 1)
            dve.wait_ge(angle_step, 12)
            dve.tensor_scalar(cos[:, :, :], angle[1], -2.0, 1.0, ALU.mult, ALU.add).then_inc(tables_ready, 1)
            dve.wait_ge(tables_ready, 2)

            def add_bias(key, uses, to, c, e):
                w = e - c
                dve.wait_ge(ring_s.full(key), uses + 1)
                dve.tensor_tensor(to, ring_s.view(key).rearrange("p (t c) -> p t c", c=w),
                                  bias_in[:, c:e].unsqueeze(1).to_broadcast([P, 2 * BANK // w, w]), ALU.add)\
                    .then_inc(ring_s.emptied(key), 1)

            def qk_rows(i, n):
                add_bias(("qk", n), ring_s.uses_ahead(("qk", n), i), qk[:, 2 * n:2 * n + 2, :], 0, QK)

            def value_rows(i, n):
                add_bias(("v", n), ring_s.uses(("v", n), i), v[:, TH * n:TH * (n + 1), :], QK, QK + D)

            def parts(i, kind, pair, c):
                key = ("parts", kind, pair, c)
                cols = slice(c * BANK, (c + 1) * BANK)
                ps = ring_of(key).view(key)
                dve.wait_ge(part_high, 16 * i + 2 * parts_order.index((kind, pair, c)) + 2)
                for hh in range(2):
                    own, other = slice(hh * HD, (hh + 1) * HD), slice((1 - hh) * HD, (2 - hh) * HD)
                    h = 2 * pair + hh
                    if kind == "q":
                        ins = dve.tensor_tensor(q_low[own, h, cols], ps[own], high(q_high[own, h, cols]),
                                                ALU.subtract)
                    else:
                        ins = dve.tensor_tensor(k_both[other, h, cols], ps[own], high(k_both[own, h, cols]),
                                                ALU.subtract)
                ins.then_inc(ring_of(key).emptied(key), 1)

            def peaks(i, g):
                key = ("s", g)
                dve.wait_ge(ring_s.full(key), ring_s.uses(key, i) + 1)
                dve.tensor_reduce(peak[:, g:g + 1], ring_s.view(key), AX.X, ALU.max).then_inc(peak_done, 1)
                dve.wait_ge(peak_done, G * i + g + 1)
                dve.tensor_scalar(shift[:, g:g + 1], peak[:, g:g + 1], -(HD ** -0.5), None, ALU.mult)\
                    .then_inc(shift_done, 1)

            def prob_turned(i, g):
                u, _, _, hh, t = step_of(g)
                key = ("p", g, 1)
                dve.wait_ge(ring_t.full(key), ring_t.uses(key, i) + 1)
                dve.tensor_copy(prob_t[u % 2][hh][:, 4:8, t * P:(t + 1) * P],
                                ring_t.view(key).rearrange("p (j t) -> p j t", t=P)).then_inc(ring_t.emptied(key), 1)

            def rows_divided(i, u):
                cols = slice(STEPS_U * u, STEPS_U * (u + 1))
                for g in (STEPS_U * u + 6, STEPS_U * u + 7):
                    dve.wait_ge(ring_s.emptied(("s", g)), ring_s.uses(("s", g), i) + 1)
                dve.reciprocal(share[:, cols], total[:, cols]).then_inc(share_done, 1)
                key = ("back", u)
                ring = ring_of(key)
                dve.wait_ge(share_done, UNITS * i + u + 1)
                dve.wait_ge(ring.full(key), ring.uses(key, i) + 1)
                dve.tensor_tensor(y_rows[:, :, :].rearrange("p t (h e) -> p t h e", e=HD),
                                  ring.view(key).rearrange("p (t h e) -> p t h e", h=2, e=HD),
                                  share[:, cols].rearrange("p (h t) -> p t h", h=2).unsqueeze(3)
                                  .to_broadcast([P, TH, 2, HD]), ALU.mult).then_inc(ring.emptied(key), 1)

            def logits(i, t):
                key = ("logits", t)
                dve.wait_ge(ring_b.full(key), ring_b.uses(key, i) + 1)
                dve.tensor_copy(f.logits[:, t, :], ring_b.view(key)[:, 0:E]).then_inc(ring_b.emptied(key), 1)

            def softmax(i):
                key = ("logits", T - 1)
                dve.wait_ge(ring_b.emptied(key), ring_b.uses(key, i) + 1)
                f.dve_softmax(dve, i - 1)

            def side(i, before, what, *at):
                if what == "parts":
                    parts(i, *at)
                elif what == "back":
                    rows_divided(i, *at)
                elif what == "out":
                    f.dve_outs(dve, ring_b, i, (what, *at), at)
                    f.dve_outs_done(dve, ring_b, i, (what, *at), at)
                    f.dve_stats2(dve, i, *at)
                elif what == "logits" and before:
                    logits(i, *at)

            def last_outs(i):
                for n in range(2):
                    f.dve_outs(dve, ring_s, i, ("out", n), (TH + 2 * n, TH + 2 * n + 1))

            def last_outs_done(i):
                for n in range(2):
                    f.dve_outs_done(dve, ring_s, i, ("out", n), (TH + 2 * n, TH + 2 * n + 1))

            def last_stats(i):
                for t in range(TH, T):
                    f.dve_stats2(dve, i, t)
                f.dve_mean2(dve, i)

            def batch(i, before, ahead):
                qk_rows(i, 0)
                if before:
                    rows_divided(i - 1, UNITS - 1)
                qk_rows(i, 1)
                rope_products(dve, i, 0, 0, (cos, sin))
                qk_rows(i, 2)
                rope_sum(dve, i, 0, 0, ALU.subtract)
                qk_rows(i, 3)
                rope_products(dve, i, 1, 0, (cos, sin))
                if before:
                    last_outs(i - 1)
                rope_sum(dve, i, 1, 0, ALU.subtract)
                if before:
                    last_outs_done(i - 1)
                for part in parts_first[:2]:
                    parts(i, *part)
                value_rows(i, 0)
                parts(i, *parts_first[2])
                value_rows(i, 1)
                if before:
                    last_stats(i - 1)
                for g in range(LAST):
                    if g < G:
                        peaks(i, g)
                    if g in beside:
                        side(i, before, *beside[g])
                    if turns_prob(g) is not None:
                        prob_turned(i, turns_prob(g))
                    if before and g == SOFTMAX:
                        softmax(i)
                    if before and g == SOFTMAX + 2:
                        f.dve_scores(dve, i - 1)
                    if ahead and stats_tiles(g) is not None:
                        f.dve_stats(dve, i + 1, stats_tiles(g))
                    if ahead and g == MEAN:
                        f.dve_mean(dve, i + 1)
                    if ahead and norm_tiles(g) is not None:
                        f.dve_norm(dve, i + 1, norm_tiles(g))
                    if ahead and turns_x(g) is not None:
                        f.dve_turn(dve, ring_s, i + 1, turns_x(g))
            batch(0, False, True)
            with dve.Fori(1, B - 1) as i:
                batch(i, True, True)
            batch(B - 1, True, False)
            rows_divided(B - 1, UNITS - 1)
            last_outs(B - 1)
            last_outs_done(B - 1)
            last_stats(B - 1)
            f.dve_norm2(dve, B - 1, range(T))
            f.dve_last_route(dve)
            f.dve_softmax(dve, B - 1)
            f.dve_scores(dve, B - 1)


def two_layers(nc, x, basis_t, w_va_t, b_va, w_oa_t, b_oa, w_q, w_k, w_v, b_q, b_k, b_v, w_o, b_o, freq,
               gate_t, wg_t, wu_t, wd_t, sg_t, su_t, sd_t, identity, causal, batch_start, position, exponent, out):
    def scratch(name, rows):
        return nc.dram_tensor(name, [rows, D], F32).ap()

    def batches(a):
        return a.rearrange("(b s) d -> b s d", s=S)

    x1, xn1, x2 = scratch("x1", B * S), scratch("xn1", B * S), scratch("x2", B * S)
    x3, xn3 = scratch("x3", B * S), scratch("xn3", B * S)
    with ExitStack() as ctx:
        ident = ctx.enter_context(nc.sbuf_tensor("ident", [P, P], F32))
        gate = ctx.enter_context(nc.sbuf_tensor("gate", [P, KD, E], F32))
        scores = ctx.enter_context(nc.sbuf_tensor("scores", [P, T, B, E], F32))
        const_loaded = ctx.enter_context(nc.semaphore("const_loaded"))
        with nc.Block() as block:
            @block.sync
            def _(sp):
                sp.dma_start(ident[:, :], identity).then_inc(const_loaded, 16)
                sp.dma_start(gate[:, :, :], gate_t.rearrange("(k p) e -> p k e", p=P)).then_inc(const_loaded, 16)
                sp.wait_ge(const_loaded, 32)
        with ExitStack() as causal_ctx:
            mask = causal_ctx.enter_context(nc.sbuf_tensor("mask", [P, 2, P], BF16))
            with nc.Block() as block:
                @block.sync
                def _(sp):
                    sp.dma_start(mask[:, :, :], causal).then_inc(const_loaded, 16)
                    sp.wait_ge(const_loaded, 48)
            attention_a(nc, x, basis_t, w_va_t, b_va, w_oa_t, b_oa, batches(x1), batches(xn1),
                        ident, mask, gate, scores)
        of_experts = {}

        def sem(name):
            if name not in of_experts:
                of_experts[name] = ctx.enter_context(nc.semaphore(f"f_{name}"))
            return of_experts[name]

        experts(nc, "f1", sem, batches(x1), xn1, wg_t, wu_t, wd_t, sg_t, su_t, sd_t, x2, ident, scores, batch_start)
        attention_b(nc, batches(x2), w_q, w_k, w_v, b_q, b_k, b_v, w_o, b_o, freq, position, exponent,
                    batches(x3), batches(xn3), ident, gate, scores)
        with nc.Block() as block:
            @block.gpsimd
            def _(pool):
                for s in of_experts.values():
                    pool.sem_clear(s)
        experts(nc, "f2", sem, batches(x3), xn3, wg_t, wu_t, wd_t, sg_t, su_t, sd_t,
                out.rearrange("b s d -> (b s) d"), ident, scores, batch_start)


_TURNED = ["L0_attn_a_W_basis", "L0_attn_a_W_v", "L0_attn_a_b_v", "L0_attn_a_W_o", "L0_attn_a_b_o",
           "L0_attn_b_Wq", "L0_attn_b_Wk", "L0_attn_b_Wv", "L0_attn_b_bq", "L0_attn_b_bk", "L0_attn_b_bv",
           "L0_attn_b_Wo", "L0_attn_b_bo", "L0_attn_b_nrope_freq",
           "L0_ffn_gate_w", "L0_ffn_Wg", "L0_ffn_Wu", "L0_ffn_Wd", "L0_ffn_Ws_g", "L0_ffn_Ws_u", "L0_ffn_Ws_d"]


def kernel(**inputs):
    import ml_dtypes as _ml
    import numpy as _np
    import concourse.bacc as _bacc
    from concourse import mybir as _mybir
    from concourse.bass_utils import run_bass_kernel_spmd as _run

    nc = _bacc.Bacc("TRN2", target_bir_lowering=False, num_devices=1)
    arrays, args = {}, []

    def give(name, a):
        a = _np.ascontiguousarray(a)
        arrays[f"in_{name}"] = a
        args.append(nc.dram_tensor(f"in_{name}", a.shape, _mybir.dt.from_np(a.dtype), kind="ExternalInput").ap())

    give("x", inputs["L0_attn_a_hidden_states"])
    for name in _TURNED:
        a = _np.asarray(inputs[name])
        turned = a.ndim > 1 and not name.startswith("L0_attn_b")
        give(name, a.swapaxes(-1, -2) if turned else a)
    give("identity", _np.eye(P, dtype=_np.float32))
    causal = _np.zeros((P, 2, P), _np.float32)
    causal[:, 0] = _np.eye(P)
    causal[:, 1][_np.triu_indices(P, 1)] = -3e38
    give("causal", causal.astype(_ml.bfloat16))
    give("batch_start", (_np.arange(P) // E * S).astype(_np.float32)[:, None])
    give("position", (_np.arange(T)[None] * P + _np.arange(P)[:, None]).astype(_np.float32))
    give("exponent", _np.tile((-_np.arange(Q4) / Q4).astype(_np.float32), (P, 1)))
    args.append(nc.dram_tensor("out", (B, S, D), F32, kind="ExternalOutput").ap())
    two_layers(nc, *args)
    r = _run(nc, [arrays], core_ids=[0])
    return r.results[0]["out"]
```
